# Optimizing a Trainium2 kernel written in Bass

```python
import numpy as np
import jax
import jax.numpy as jnp

def _softmax(x, axis=-1):
    return jax.nn.softmax(x, axis=axis)

def _gelu(x):
    return jax.nn.gelu(x, approximate=True)

def _silu(x):
    return jax.nn.silu(x)

def _sigmoid(x):
    return jax.nn.sigmoid(x)

def _layernorm(x, axis=-1, eps=1e-05):
    m = jnp.mean(x, axis=axis, keepdims=True)
    v = jnp.var(x, axis=axis, keepdims=True)
    return (x - m) / jnp.sqrt(v + eps)

def _scatter_add(tgt, idx, src, axis=0):
    return tgt.at[idx].add(src)

def _segment_sum(src, seg, n):
    return jax.ops.segment_sum(src, seg, n)
kernel_name = 'mk_prb_d1_jaxref_r8_3e673c'

def setup_inputs(seed: int=0):
    np.random.seed(seed)
    _w = jnp.asarray

    def _L0_attn_setup():
        import jax, jax.numpy as jnp
        from jax import lax
        import numpy as np
        D_MODEL, D_STATE, D_CONV, EXPAND = (128, 16, 4, 2)
        D_INNER = EXPAND * D_MODEL
        DT_RANK = (D_MODEL + 15) // 16
        B, L = (2, 256)

        def layernorm(x, g, b, eps=1e-05):
            mu = jnp.mean(x, -1, keepdims=True)
            var = jnp.mean((x - mu) ** 2, -1, keepdims=True)
            return (x - mu) * lax.rsqrt(var + eps) * g + b

        def mamba(x, in_w, conv_w, conv_b, x_w, dt_w, dt_b, A_log, Dp, out_w):
            Bb, Ll, _ = x.shape
            xz = x @ in_w.T
            xi, z = jnp.split(xz, 2, axis=-1)
            xc = jnp.transpose(xi, (0, 2, 1))
            xc = lax.conv_general_dilated(xc, conv_w[:, None, :], (1,), [(D_CONV - 1, 0)], dimension_numbers=('NCH', 'OIH', 'NCH'), feature_group_count=D_INNER)
            xc = xc + conv_b[None, :, None]
            xi = jax.nn.silu(jnp.transpose(xc, (0, 2, 1)))
            dbc = xi @ x_w.T
            dt, Bm, Cm = jnp.split(dbc, [DT_RANK, DT_RANK + D_STATE], axis=-1)
            delta = jax.nn.softplus(dt @ dt_w.T + dt_b)
            A = -jnp.exp(A_log)

            def step(h, inp):
                d_t, B_t, C_t, u_t = inp
                dA = jnp.exp(d_t[..., None] * A)
                h = h * dA + (d_t * u_t)[..., None] * B_t[:, None, :]
                y = jnp.einsum('bdn,bn->bd', h, C_t)
                return (h, y)
            h0 = jnp.zeros((Bb, D_INNER, D_STATE), x.dtype)
            _, ys = lax.scan(step, h0, (jnp.swapaxes(delta, 0, 1), jnp.swapaxes(Bm, 0, 1), jnp.swapaxes(Cm, 0, 1), jnp.swapaxes(xi, 0, 1)))
            y = jnp.swapaxes(ys, 0, 1) + xi * Dp
            y = y * jax.nn.silu(z)
            return y @ out_w.T
        key = jax.random.key(seed)
        ks = jax.random.split(key, 20)
        s = lambda fan: 1.0 / np.sqrt(fan)

        def mamba_params(k):
            kk = jax.random.split(k, 8)
            return dict(in_w=jax.random.normal(kk[0], (2 * D_INNER, D_MODEL)) * s(D_MODEL), conv_w=jax.random.normal(kk[1], (D_INNER, D_CONV)) * s(D_CONV), conv_b=jnp.zeros((D_INNER,)), x_w=jax.random.normal(kk[2], (DT_RANK + 2 * D_STATE, D_INNER)) * s(D_INNER), dt_w=jax.random.normal(kk[3], (D_INNER, DT_RANK)) * s(DT_RANK), dt_b=jax.random.normal(kk[4], (D_INNER,)) * 0.1, A_log=jnp.log(jnp.arange(1, D_STATE + 1, dtype=jnp.float32))[None, :] * jnp.ones((D_INNER, 1)), D=jnp.ones((D_INNER,)), out_w=jax.random.normal(kk[5], (D_MODEL, D_INNER)) * s(D_INNER))
        f = mamba_params(ks[1])
        b = mamba_params(ks[2])
        inp = {'x': jax.random.normal(ks[0], (B, L, D_MODEL)), 'ln_g': jnp.ones((D_MODEL,)), 'ln_b': jnp.zeros((D_MODEL,)), 'combine_w': jax.random.normal(ks[3], (D_MODEL, 2 * D_MODEL)) * s(2 * D_MODEL), 'combine_b': jnp.zeros((D_MODEL,))}
        for name, p in (('f', f), ('b', b)):
            for k2, v in p.items():
                inp[f'{name}_{k2}'] = v
        return inp
    _L0_attn_in = _L0_attn_setup()

    def _L0_ffn_setup():
        import jax, jax.numpy as jnp
        import numpy as np
        S, B, H, I, E = (64, 2, 128, 352, 8)
        key = jax.random.key(seed)
        ks = jax.random.split(key, 5)
        return {'hidden_states': jax.random.normal(ks[0], (S, B, H), dtype=jnp.float32), 'router_w': jax.random.normal(ks[1], (E, H), dtype=jnp.float32) * 0.02, 'gate_w': jax.random.normal(ks[2], (E, I, H), dtype=jnp.float32) * 0.02, 'up_w': jax.random.normal(ks[3], (E, I, H), dtype=jnp.float32) * 0.02, 'down_w': jax.random.normal(ks[4], (E, H, I), dtype=jnp.float32) * 0.02}
    _L0_ffn_in = _L0_ffn_setup()
    _d = {'L0_attn_x': _L0_attn_in['x'], 'L0_attn_ln_g': _L0_attn_in['ln_g'], 'L0_attn_ln_b': _L0_attn_in['ln_b'], 'L0_attn_combine_w': _L0_attn_in['combine_w'], 'L0_attn_combine_b': _L0_attn_in['combine_b'], 'L0_attn_f_in_w': _L0_attn_in['f_in_w'], 'L0_attn_f_conv_w': _L0_attn_in['f_conv_w'], 'L0_attn_f_conv_b': _L0_attn_in['f_conv_b'], 'L0_attn_f_x_w': _L0_attn_in['f_x_w'], 'L0_attn_f_dt_w': _L0_attn_in['f_dt_w'], 'L0_attn_f_dt_b': _L0_attn_in['f_dt_b'], 'L0_attn_f_A_log': _L0_attn_in['f_A_log'], 'L0_attn_f_D': _L0_attn_in['f_D'], 'L0_attn_f_out_w': _L0_attn_in['f_out_w'], 'L0_attn_b_in_w': _L0_attn_in['b_in_w'], 'L0_attn_b_conv_w': _L0_attn_in['b_conv_w'], 'L0_attn_b_conv_b': _L0_attn_in['b_conv_b'], 'L0_attn_b_x_w': _L0_attn_in['b_x_w'], 'L0_attn_b_dt_w': _L0_attn_in['b_dt_w'], 'L0_attn_b_dt_b': _L0_attn_in['b_dt_b'], 'L0_attn_b_A_log': _L0_attn_in['b_A_log'], 'L0_attn_b_D': _L0_attn_in['b_D'], 'L0_attn_b_out_w': _L0_attn_in['b_out_w'], 'L0_ffn_router_w': _L0_ffn_in['router_w'], 'L0_ffn_gate_w': _L0_ffn_in['gate_w'], 'L0_ffn_up_w': _L0_ffn_in['up_w'], 'L0_ffn_down_w': _L0_ffn_in['down_w']}
    _x0 = _d['L0_attn_x']
    _d['L0_attn_x'] = jax.random.normal(jax.random.fold_in(jax.random.key(seed), 1), (8, 512, 128), dtype=_x0.dtype)
    del _x0
    return _d

def reference(L0_attn_x, L0_attn_ln_g, L0_attn_ln_b, L0_attn_combine_w, L0_attn_combine_b, L0_attn_f_in_w, L0_attn_f_conv_w, L0_attn_f_conv_b, L0_attn_f_x_w, L0_attn_f_dt_w, L0_attn_f_dt_b, L0_attn_f_A_log, L0_attn_f_D, L0_attn_f_out_w, L0_attn_b_in_w, L0_attn_b_conv_w, L0_attn_b_conv_b, L0_attn_b_x_w, L0_attn_b_dt_w, L0_attn_b_dt_b, L0_attn_b_A_log, L0_attn_b_D, L0_attn_b_out_w, L0_ffn_router_w, L0_ffn_gate_w, L0_ffn_up_w, L0_ffn_down_w):

    def _L0_attn_ref(x, ln_g, ln_b, combine_w, combine_b, f_in_w, f_conv_w, f_conv_b, f_x_w, f_dt_w, f_dt_b, f_A_log, f_D, f_out_w, b_in_w, b_conv_w, b_conv_b, b_x_w, b_dt_w, b_dt_b, b_A_log, b_D, b_out_w):
        import jax, jax.numpy as jnp
        from jax import lax
        import numpy as np
        D_MODEL, D_STATE, D_CONV, EXPAND = (128, 16, 4, 2)
        D_INNER = EXPAND * D_MODEL
        DT_RANK = (D_MODEL + 15) // 16
        B, L = (2, 256)

        def layernorm(x, g, b, eps=1e-05):
            mu = jnp.mean(x, -1, keepdims=True)
            var = jnp.mean((x - mu) ** 2, -1, keepdims=True)
            return (x - mu) * lax.rsqrt(var + eps) * g + b

        def mamba(x, in_w, conv_w, conv_b, x_w, dt_w, dt_b, A_log, Dp, out_w):
            Bb, Ll, _ = x.shape
            xz = x @ in_w.T
            xi, z = jnp.split(xz, 2, axis=-1)
            xc = jnp.transpose(xi, (0, 2, 1))
            xc = lax.conv_general_dilated(xc, conv_w[:, None, :], (1,), [(D_CONV - 1, 0)], dimension_numbers=('NCH', 'OIH', 'NCH'), feature_group_count=D_INNER)
            xc = xc + conv_b[None, :, None]
            xi = jax.nn.silu(jnp.transpose(xc, (0, 2, 1)))
            dbc = xi @ x_w.T
            dt, Bm, Cm = jnp.split(dbc, [DT_RANK, DT_RANK + D_STATE], axis=-1)
            delta = jax.nn.softplus(dt @ dt_w.T + dt_b)
            A = -jnp.exp(A_log)

            def step(h, inp):
                d_t, B_t, C_t, u_t = inp
                dA = jnp.exp(d_t[..., None] * A)
                h = h * dA + (d_t * u_t)[..., None] * B_t[:, None, :]
                y = jnp.einsum('bdn,bn->bd', h, C_t)
                return (h, y)
            h0 = jnp.zeros((Bb, D_INNER, D_STATE), x.dtype)
            _, ys = lax.scan(step, h0, (jnp.swapaxes(delta, 0, 1), jnp.swapaxes(Bm, 0, 1), jnp.swapaxes(Cm, 0, 1), jnp.swapaxes(xi, 0, 1)))
            y = jnp.swapaxes(ys, 0, 1) + xi * Dp
            y = y * jax.nn.silu(z)
            return y @ out_w.T
        residual = x
        xn = layernorm(x, ln_g, ln_b)
        out_f = mamba(xn, f_in_w, f_conv_w, f_conv_b, f_x_w, f_dt_w, f_dt_b, f_A_log, f_D, f_out_w)
        out_b = mamba(xn[:, ::-1], b_in_w, b_conv_w, b_conv_b, b_x_w, b_dt_w, b_dt_b, b_A_log, b_D, b_out_w)[:, ::-1]
        out = jnp.concatenate([out_f, out_b], axis=-1) @ combine_w.T + combine_b
        return out + residual

    def _L0_ffn_ref(hidden_states, router_w, gate_w, up_w, down_w):
        import jax, jax.numpy as jnp
        import numpy as np
        S, B, H, I, E = (64, 2, 128, 352, 8)
        router_logits = jnp.einsum('sbh,eh->sbe', hidden_states, router_w)
        routing_indices = jnp.argmax(router_logits, axis=-1)
        out = jnp.zeros_like(hidden_states)
        for e in range(E):
            mask = (routing_indices == e)[..., None]
            xe = jnp.where(mask, hidden_states, 0.0)
            g = jnp.einsum('sbh,ih->sbi', xe, gate_w[e])
            u = jnp.einsum('sbh,ih->sbi', xe, up_w[e])
            ye = jnp.einsum('sbi,hi->sbh', jax.nn.silu(g) * u, down_w[e])
            out = out + jnp.where(mask, ye, 0.0)
        return out
    x = L0_attn_x
    xn = _layernorm(x, axis=-1)
    x = x + _L0_attn_ref(xn, L0_attn_ln_g, L0_attn_ln_b, L0_attn_combine_w, L0_attn_combine_b, L0_attn_f_in_w, L0_attn_f_conv_w, L0_attn_f_conv_b, L0_attn_f_x_w, L0_attn_f_dt_w, L0_attn_f_dt_b, L0_attn_f_A_log, L0_attn_f_D, L0_attn_f_out_w, L0_attn_b_in_w, L0_attn_b_conv_w, L0_attn_b_conv_b, L0_attn_b_x_w, L0_attn_b_dt_w, L0_attn_b_dt_b, L0_attn_b_A_log, L0_attn_b_D, L0_attn_b_out_w) + _L0_ffn_ref(xn, L0_ffn_router_w, L0_ffn_gate_w, L0_ffn_up_w, L0_ffn_down_w)
    return x

_drawn_inputs = setup_inputs


def setup_inputs(seed=0):
    import zlib

    import numpy as np

    out = dict(_drawn_inputs(seed))
    spreads = {'L0_attn_ln_g': (1.0, 0.2),
     'L0_attn_ln_b': (0.0, 0.367),
     'L0_attn_combine_b': (0.0, 0.596),
     'L0_attn_f_conv_b': (0.0, 0.7),
     'L0_attn_f_D': (1.0, 0.573),
     'L0_attn_b_conv_b': (0.0, 0.688),
     'L0_attn_b_D': (1.0, 0.6)}
    factors = {'L0_attn_f_dt_b': 13.412,
     'L0_attn_b_dt_b': 13.769,
     'L0_ffn_router_w': 8.0,
     'L0_ffn_gate_w': 8.0,
     'L0_ffn_up_w': 8.0,
     'L0_ffn_down_w': 8.0,
     'L0_attn_f_A_log': 6.144,
     'L0_attn_b_A_log': 4.557}
    for name, (base, spread) in spreads.items():
        noise = np.random.default_rng([zlib.crc32(name.encode()), seed]).standard_normal(out[name].shape)
        drawn = base * np.exp(spread * noise) if base else spread * noise
        out[name] = jnp.asarray(drawn.astype(out[name].dtype))
    for name, factor in factors.items():
        out[name] = (out[name] * factor).astype(out[name].dtype)
    return out
```

```python
from contextlib import ExitStack

import concourse.bass as bass
from concourse import mybir

F32 = mybir.dt.float32
I32 = mybir.dt.int32
U32 = mybir.dt.uint32
ALU = mybir.AluOpType
ACT = mybir.ActivationFunctionType
AX_X = mybir.AxisListType.X

P = 128
NB, L, H = 8, 512, 128
KB = L // P
NBLK = NB * KB
DI, DS, DR, NTAP = 256, 16, 8, 4
NDBC = DR + 2 * DS
G, DD = 4, 32
R = DS // G
J = DI // DD
RH = 2
NSTEP = J * R // RH
UNITS = 2 * NB
E, IF, IFP = 8, 352, 384
NCH = IFP // P
NTILE = NBLK + E - 1
EPS = 1e-5

C_ID, C_TRI, C_SEL, C_IOTA, C_THR, C_NOTFIRST, C_TILE = 0, 128, 256, 288, 296, 328, 584
C_END = C_TILE + NTILE


class Flow:

    def __init__(self, sem):
        self.sem, self.value = sem, 0


class Queue:

    def __init__(self, own):
        self.ops, self.own, self.met = [], own, {}

    def wait(self, *marks):
        for mark in marks:
            if mark is None:
                continue
            flow, value = mark
            if self.met.get(id(flow), 0) >= value:
                continue
            self.met[id(flow)] = value
            self.ops.append(lambda e, s=flow.sem, v=value: e.wait_ge(s, v))

    def run(self, fn, signal=True, flow=None, by=1):
        if not signal:
            self.ops.append(fn)
            return None
        flow = flow or self.own
        flow.value += by
        self.ops.append(lambda e: fn(e).then_inc(flow.sem, by))
        return flow, flow.value

    def play(self, e):
        for op in self.ops:
            op(e)


def mamba_moe_kernel(nc, x, in_wT, conv_wT, conv_b, x_wT, dt_wT, dt_b, A_log, Dp, out_w, comb_wT, comb_b,
                     ln_g, ln_b, router_wT, gate_up, down, consts, out):
    ctx = ExitStack()
    with ctx:
        def sb(name, shape, dt=F32):
            return ctx.enter_context(nc.sbuf_tensor(name, shape, dt))

        def flow(name):
            return Flow(ctx.enter_context(nc.semaphore(name)))

        def dram(name, shape, dt=F32):
            return nc.dram_tensor(name, shape, dt, kind="Internal").ap()

        xn_d = dram("xn_scratch", (NBLK * P, H))
        xn2_d = dram("xn2_scratch", (NBLK * P, H))
        base_d = dram("base_scratch", (NBLK * P, H))
        attn_d = dram("attn_scratch", (NBLK * P, H))
        sorted_d = dram("sorted_tokens", (NTILE * P, H))
        ffn_d = dram("sorted_ffn", (NTILE * P, H))
        delta_d = dram("delta_scratch", (2, DD, J, L))
        du_d = dram("du_scratch", (2, DD, J, L))
        dbc_d = dram("dbc_scratch", (2, NDBC, L))

        def by_batch(t, b):
            return t.rearrange("(b k p) h -> b p k h", b=NB, p=P)[b]

        cst = sb("cst", [P, C_END])
        ones = sb("ones", [P, P])
        neg_half = sb("neg_half", [P, KB])
        w_in = sb("w_in", [P, 2, NTAP + 1, DI])
        w_x = sb("w_x", [P, 2, 2, NDBC])
        w_dt = sb("w_dt", [DR, 2, DI])
        diag_D = sb("diag_D", [P, 2, 2, P])
        w_out = sb("w_out", [P, 2, 2, H])
        cols = sb("cols", [P, 16])
        A_sb = sb("A_sb", [P, 2, J, R])
        rw = sb("rw", [P, E])
        comb_bias = sb("comb_bias", [P, H])
        xt = sb("xt", [P, KB, H])
        xn = sb("xn", [P, KB, H])
        xn2 = sb("xn2", [P, KB, H])
        stats = sb("stats", [P, KB, 6])
        moments = sb("moments", [P, KB, 2])
        rstd = sb("rstd", [P, KB])
        rstd2 = sb("rstd2", [P, KB])
        xnT = sb("xnT", [P, L])
        xn2_in = sb("xn2_in", [P, KB, H])
        xpad = sb("xpad", [P, 2, L + 6])
        xi = sb("xi", [P, 2, 2, L])
        tmpA = sb("tmpA", [P, 2, L])
        tmpB = sb("tmpB", [P, 2, L])
        du = tmpB
        zs = sb("zs", [P, 2, 2, L])
        dbc = sb("dbc", [NDBC, L])
        NP = 4
        delta_rep = sb("delta_rep", [P, NP, 2, L])
        du_rep = sb("du_rep", [P, NP, 2, L])
        B_rep = sb("B_rep", [P, 2, R, L])
        C_rep = sb("C_rep", [P, 2, R, L])
        NA, NH, LEAD = 4, 6, 3
        dA = sb("dA", [P, NA, RH * L + 1])
        hs = sb("hs", [P, NH, RH * L])
        yg = sb("yg", [P, 2, 2, L])
        base_in = sb("base_in", [P, KB, H])
        NW = 3
        gu_w = sb("gu_w", [P, NW, 2, IFP])
        dn_w = sb("dn_w", [P, NW, NCH, H])
        xs = sb("xs", [P, 2, H])
        xsT = sb("xsT", [P, 2, P])
        th_f = sb("th_f", [P, 2, IFP])
        act_f = sb("act_f", [P, 2, IFP])
        ys = sb("ys", [P, 2, H])
        fin = (xt, xn)
        attn_in = sb("attn_in", [P, 2, KB, H])
        logits = sb("logits", [P, NBLK, E])
        pos_u = sb("pos_u", [P, NBLK], U32)
        ej_i = sb("ej_i", [P, NTILE], I32)
        small = sb("small", [P, 64])

        def bank(name):
            return ctx.enter_context(nc.psum_tensor(name, [P, 512], F32))

        Y = [bank("y0"), bank("y1")]
        FB = [bank("front0"), bank("front1")]
        MB = bank("mixed")
        GB, UB, TB = bank("gate"), bank("up"), bank("turn")

        pe, act, dve, pool, sp = (Queue(flow("done_" + n)) for n in ("pe", "act", "dve", "pool", "sp"))
        fl = {}

        def dma(dst, src, name, k=0, q=None):
            key = f"dma_{name}{k}"
            if key not in fl:
                fl[key] = flow(key)
            return (q or sp).run(lambda e: e.dma_start(dst, src), flow=fl[key], by=16)

        t = {}

        ident = cst[:, C_ID:C_ID + P]
        tri = cst[:, C_TRI:C_TRI + P]
        sel = cst[:, C_SEL:C_SEL + DD]

        t["cst"] = dma(cst[:, :], consts, "w")
        cwb = delta_rep[:, :, :, :].rearrange("p a b c -> p (a b c)")[:, 0:2 * NTAP * DI].rearrange(
            "p (d k c) -> p d k c", d=2, k=NTAP)
        inw_t = du_rep[:, :, :, :].rearrange("p a b c -> p (a b c)")[:, 0:2 * 2 * DI].rearrange(
            "p (d c) -> p d c", d=2)
        outw_t = hs[:, 0, 0:2 * DI].rearrange("p (d c) -> p d c", d=2)
        combw_t = hs[:, 1, 0:2 * H].rearrange("p (d o) -> p d o", d=2)
        for d in range(2):
            dma(cwb[:, d, :, :], conv_wT[d].rearrange("k c -> (k c)").unsqueeze(0).broadcast_to([P, NTAP * DI]), "w")
            dma(inw_t[:, d, :], in_wT[d], "w")
            dma(w_x[:, d, :, :], x_wT[d], "w")
            dma(w_dt[:, d, :], dt_wT[d], "w")
            dma(cols[:, 2 * d:2 * d + 2], conv_b[d], "w")
            dma(cols[:, 4 + 2 * d:6 + 2 * d], dt_b[d], "w")
            dma(cols[:, 8 + 2 * d:10 + 2 * d], Dp[d], "w")
            dma(A_sb[:, d, :, :], A_log[d], "w")
            dma(outw_t[:, d, :], out_w[d], "w")
            dma(combw_t[:, d, :], comb_wT[:, d, :], "w")
        dma(cols[:, 12:13], ln_g, "w")
        dma(cols[:, 13:14], ln_b, "w")
        dma(rw[:, :], router_wT, "w")
        weights_in = dma(comb_bias[:, :], comb_b.broadcast_to([P, H]), "w")

        def conv_bias(d, h):
            return cols[:, 2 * d + h:2 * d + h + 1]

        def dt_bias(d, h):
            return cols[:, 4 + 2 * d + h:5 + 2 * d + h]

        t["ones"] = dve.run(lambda e: e.memset(ones[:, :], 1.0))
        t["pow"] = dve.run(lambda e: e.memset(neg_half[:, :], -0.5))
        t["xpad0"] = dve.run(lambda e: e.memset(xpad[:, :, :], 0.0))
        t["dA0"] = dve.run(lambda e: e.memset(dA[:, :, :], 0.0))
        t["sorted0"] = dve.run(lambda e: e.memset(act_f[:, :, :], 0.0))

        dve.wait(weights_in)
        for d in range(2):
            t["w_in"] = dve.run(lambda e, d=d: e.scalar_tensor_tensor(
                w_in[:, d, 0:NTAP, :], inw_t[:, d, 0:DI].unsqueeze(1).broadcast_to([P, NTAP, DI]), 0.5,
                cwb[:, d, :, :], ALU.mult, ALU.mult))
            t["w_in"] = dve.run(lambda e, d=d: e.tensor_scalar(
                w_in[:, d, NTAP, :], inw_t[:, d, DI:2 * DI], 0.5, None, ALU.mult))
            for h in range(2):
                t["diag"] = dve.run(lambda e, d=d, h=h: e.tensor_scalar(
                    diag_D[:, d, h, :], ident, cols[:, 8 + 2 * d + h:9 + 2 * d + h], None, ALU.mult))
        t["conv_bias"] = dve.run(lambda e: e.tensor_scalar(cols[:, 0:4], cols[:, 0:4], 0.5, None, ALU.mult))
        act.wait(weights_in)
        a1 = act.run(lambda e: e.activation(A_sb[:, :, :, :], A_sb[:, :, :, :], ACT.Exp))
        dve.wait(a1)
        t["A"] = dve.run(lambda e: e.tensor_scalar(A_sb[:, :, :, :], A_sb[:, :, :, :], -1.0, None, ALU.mult))
        pe.wait(weights_in)
        for d in range(2):
            for h in range(2):
                m = pe.run(lambda e, d=d, h=h: e.matmul(
                    MB[:, (2 * d + h) * H:(2 * d + h + 1) * H], outw_t[:, d, h * P:(h + 1) * P],
                    combw_t[:, d, :], start=True, stop=True))
        dve.wait(m)
        t["w_out"] = dve.run(lambda e: e.tensor_copy(
            w_out[:, :, :, :].rearrange("p d h o -> p (d h o)"), MB[:, :]))
        t["MB free"] = t["w_out"]
        t["staging"] = t["w_out"]

        def moments_of(src, mark, r):
            dve.wait(mark)
            for k in range(KB):
                s = dve.run(lambda e, k=k: e.bn_stats(stats[:, k, :], src[:, k, :]))
            dve.wait(s)
            for k in range(KB):
                m = dve.run(lambda e, k=k: e.bn_aggr(moments[:, k, :], stats[:, k, :]))
            pool.wait(m, t["pow"])
            v = pool.run(lambda e: e.tensor_scalar(r[:, :], moments[:, :, 1], EPS, None, ALU.add))
            pool.wait(v)
            return pool.run(lambda e: e.tensor_tensor(r[:, :], r[:, :], neg_half[:, :], ALU.pow))

        def normalize(dst, src, r):
            for k in range(KB):
                m = dve.run(lambda e, k=k: e.tensor_scalar(
                    dst[:, k, :], src[:, k, :], moments[:, k, 0:1], r[:, k:k + 1], ALU.subtract, ALU.mult))
            return m

        def ln_load(c):
            sp.wait(t.get("xt free"))
            t["xt"] = dma(xt[:, :, :], by_batch(x, c), "xt")

        def ln_first(c):
            t["rstd"] = moments_of(xt, t["xt"], rstd)

        def ln_second(c):
            dve.wait(t["rstd"], t.get("xn stored"), t.get("xn read"))
            t["xn"] = normalize(xn, xt, rstd)
            t["rstd2"] = moments_of(xn, t["xn"], rstd2)
            pool.wait(t["xn"], weights_in)
            b1 = pool.run(lambda e: e.tensor_tensor(xt[:, :, :], xt[:, :, :], xn[:, :, :], ALU.add))
            pool.wait(b1)
            t["base"] = pool.run(lambda e: e.tensor_tensor(
                xt[:, :, :], xt[:, :, :], comb_bias[:, :].unsqueeze(1).broadcast_to([P, KB, H]), ALU.add))
            sp.wait(t["xn"])
            t["xn stored"] = dma(by_batch(xn_d, c), xn[:, :, :], "xnout")
            sp.wait(t["base"])
            t["xt free"] = dma(by_batch(base_d, c), xt[:, :, :], "baseout")
            t["base stored", c] = t["xt free"]
            pe.wait(t["xn"], t["cst"], t.get("TB free"))
            for k in range(KB):
                m = pe.run(lambda e, k=k: e.transpose(TB[:, k * P:(k + 1) * P], xn[:, k, :], ident))
            t["xn read"] = m
            act.wait(m, t.get("logits mm"))
            t["xnT"] = act.run(lambda e: e.copy(xnT[:, :], TB[:, :]))

        def ln_third(c):
            dve.wait(t["rstd2"], t.get("xn2 stored"))
            m = normalize(xn2, xn, rstd2)
            t["xn read"] = m
            sp.wait(m)
            t["xn2 stored"] = dma(by_batch(xn2_d, c), xn2[:, :, :], "xn2out")
            t["xn2 in dram", c] = t["xn2 stored"]
            pe.wait(t["xnT"])
            for k in range(KB):
                m = pe.run(lambda e, k=k: e.matmul(TB[:, k * E:(k + 1) * E], xnT[:, k * P:(k + 1) * P], rw[:, :],
                                                   start=True, stop=True))
            t["logits mm"] = m
            act.wait(m)
            t["TB free"] = act.run(lambda e: e.copy(
                logits[:, c * KB:(c + 1) * KB, :].rearrange("p k e -> p (k e)"), TB[:, 0:KB * E]))
            t["logits"] = t["TB free"]

        def batch_load(b):
            sp.wait(t["xn2 in dram", b], t.get("xn2_in free"))
            t["xn2_in"] = dma(xn2_in[:, :, :], by_batch(xn2_d, b), "xn2in")

        def batch_turn(b):
            pe.wait(t["xn2_in"], t["cst"], t.get(("FB free", 0)))
            for k in range(KB):
                m = pe.run(lambda e, k=k: e.transpose(FB[0][:, k * P:(k + 1) * P], xn2_in[:, k, :], ident))
            t["xn2_in free"] = m
            act.wait(m, t["xpad0"], weights_in, t.get(("in proj", 2 * b - 3)))
            t["xpad", b] = act.run(lambda e: e.activation(
                xpad[:, b % 2, 3:3 + L], FB[0][:, :], ACT.Identity, scale=cols[:, 12:13], bias=cols[:, 13:14]))
            t["FB free", 0] = t["xpad", b]

        def in_proj(v, h):
            b, d = divmod(v, 2)
            pe.wait(t["xpad", b], t["w_in"], t.get(("FB free", 1 - h)))
            for k in range(NTAP):
                at = k if d == 0 else 2 * (NTAP - 1) - k
                m = pe.run(lambda e, k=k, at=at: e.matmul(
                    FB[1 - h][:, :], w_in[:, d, k, h * P:(h + 1) * P], xpad[:, b % 2, at:at + L],
                    start=(k == 0), stop=(k == NTAP - 1)), signal=k == NTAP - 1)
            t["in", v, h] = m

        def z_proj(v, h):
            b, d = divmod(v, 2)
            pe.wait(t["FB free", 1 - h])
            t["z", v, h] = pe.run(lambda e: e.matmul(
                FB[1 - h][:, :], w_in[:, d, NTAP, h * P:(h + 1) * P], xpad[:, b % 2, 3:3 + L],
                start=True, stop=True))
            t["in proj", v] = t["z", v, h]

        def xi_act(v, h):
            act.wait(t["in", v, h], t["conv_bias"], t.get(("delta stored", v - 1)), t.get(("du made", v - 1)))
            act.run(lambda e: e.activation(tmpA[:, h, :], FB[1 - h][:, :], ACT.Identity,
                                           bias=conv_bias(v % 2, h)), signal=False)
            t["th", v, h] = act.run(lambda e: e.activation(tmpB[:, h, :], FB[1 - h][:, :], ACT.Tanh,
                                                           bias=conv_bias(v % 2, h)))
            t["FB free", 1 - h] = t["th", v, h]

        def xi_mul(v, h):
            dve.wait(t["th", v, h], t.get(("D mm", v - 2)), t.get(("du made", v - 1)))
            t["xi", v, h] = dve.run(lambda e: e.scalar_tensor_tensor(
                xi[:, v % 2, h, :], tmpB[:, h, :], 1.0, tmpA[:, h, :], ALU.add, ALU.mult))

        def z_act(v, h):
            act.wait(t["z", v, h], t["xi", v, h])
            t["thz", v, h] = act.run(lambda e: e.activation(tmpB[:, h, :], FB[1 - h][:, :], ACT.Tanh))

        def z_mul(v, h):
            dve.wait(t["thz", v, h])
            t["zs", v, h] = dve.run(lambda e: e.scalar_tensor_tensor(
                zs[:, v % 2, h, :], tmpB[:, h, :], 1.0, FB[1 - h][:, :], ALU.add, ALU.mult))
            t["FB free", 1 - h] = t["zs", v, h]

        def x_proj(v):
            d = v % 2
            pe.wait(t["xi", v, 0], t["xi", v, 1], weights_in, t["MB free"])
            for h in range(2):
                m = pe.run(lambda e, h=h: e.matmul(MB[0:NDBC, :], w_x[:, d, h, :], xi[:, v % 2, h, :],
                                                   start=(h == 0), stop=(h == 1)), signal=h == 1)
            t["dbc mm"] = m

        def dbc_out(v):
            act.wait(t["dbc mm"], t.get("dbc stored"), t.get(("dt", v - 1, 1)))
            t["dbc"] = act.run(lambda e: e.copy(dbc[:, :], MB[0:NDBC, :]))
            t["MB free"] = t["dbc"]
            sp.wait(t["dbc"], t.get(("BC", v - 2)))
            t["dbc stored"] = dma(dbc_d[v % 2], dbc[:, :], "dbcout")

        def dt_proj(v):
            d = v % 2
            pe.wait(t["dbc"])
            for h in range(2):
                pe.wait(t["FB free", 1 - h])
                t["dt", v, h] = pe.run(lambda e, h=h: e.matmul(
                    FB[1 - h][:, :], w_dt[:, d, h * P:(h + 1) * P], dbc[0:DR, :], start=True, stop=True))

        def softplus_max(v):
            for h in range(2):
                dve.wait(t["dt", v, h], t["xi", v, h])
                t["m", v, h] = dve.run(lambda e, h=h: e.tensor_scalar(
                    tmpA[:, h, :], FB[1 - h][:, :], dt_bias(v % 2, h), 0.0, ALU.add, ALU.max))

        def softplus_log(v):
            for h in range(2):
                act.wait(t["m", v, h], t["zs", v, h])
                m = act.run(lambda e, h=h: e.activation(tmpB[:, h, :], FB[1 - h][:, :], ACT.Abs,
                                                        bias=dt_bias(v % 2, h)))
                t["FB free", 1 - h] = m
            act.wait(m)
            m = act.run(lambda e: e.activation(tmpB[:, :, :], tmpB[:, :, :], ACT.Exp, scale=-1.0))
            act.wait(m)
            t["log", v] = act.run(lambda e: e.activation(tmpB[:, :, :], tmpB[:, :, :], ACT.Ln, bias=1.0))

        def BC_load(v):
            k = v % 2
            sp.wait(t["dbc stored"], t.get(("mult", v - 2, NSTEP - 1)), t.get(("C mult", v - 2, NSTEP - 1)))
            for dst, row in ((B_rep, DR), (C_rep, DR + DS)):
                t["BC", v] = dma(dst[:, k, :, :].rearrange("p r t -> p (r t)"),
                                 dbc_d[k, row:row + DS, :].rearrange("(g r) t -> g (r t)", g=G)
                                 .unsqueeze(1).broadcast_to([G, DD, R * L]), "bc", k)

        def delta_out(v):
            k = v % 2
            pool.wait(t["log", v])
            t["delta", v] = pool.run(lambda e: e.tensor_tensor(tmpA[:, :, :], tmpA[:, :, :], tmpB[:, :, :],
                                                               ALU.add))
            pool.wait(t["delta", v], t["xi", v, 0], t["xi", v, 1], t.get(("du stored", v - 1)))
            t["du made", v] = pool.run(lambda e: e.tensor_tensor(du[:, :, :], tmpA[:, :, :], xi[:, k, :, :],
                                                                 ALU.mult))
            sp.wait(t["delta", v], t.get(("pair", 4 * (v - 2) + 3)))
            for h in range(2):
                t["delta stored", v] = dma(
                    delta_d[k].rearrange("e j t -> j e t")[4 * h:4 * h + 4], tmpA[:, h, :], "dout")
            sp.wait(t["du made", v])
            for h in range(2):
                t["du stored", v] = dma(
                    du_d[k].rearrange("e j t -> j e t")[4 * h:4 * h + 4], du[:, h, :], "dout")
            t["delta stored", v] = t["du stored", v]

        def pair_load(v, p):
            k, q = v % 2, 4 * v + p
            sp.wait(t["du stored", v], t.get(("pair used", q - NP)), t["staging"], t["w_in"])
            for dst, src in ((delta_rep, delta_d), (du_rep, du_d)):
                t["pair", q] = dma(dst[:, q % NP, :, :].rearrange("p j t -> p (j t)"),
                                   src[k, :, 2 * p:2 * p + 2, :].rearrange("e j t -> e (j t)")
                                   .unsqueeze(0).broadcast_to([G, DD, 2 * L]), "pair", q % NP)

        def place(s):
            return s // 4, (s // 2) % 2, s % 2

        def decay(u, s):
            p, rh, jj = place(s)
            m, q, d = NSTEP * u + s, 4 * u + p, u % 2
            act.wait(t["pair", q], t["A"], t["dA0"], t.get(("scan", m - NA)))
            src = delta_rep[:, q % NP, jj, 1:L] if d == 0 else delta_rep[:, q % NP, jj, 0:L - 1]
            for r in range(RH):
                i = act.run(lambda e, r=r: e.activation(
                    dA[:, m % NA, r * L + 1:(r + 1) * L], src, ACT.Exp,
                    scale=A_sb[:, d, 2 * p + jj, RH * rh + r:RH * rh + r + 1]), signal=r == RH - 1)
            t["decay", m] = i

        def du_B(u, s):
            p, rh, jj = place(s)
            m, q = NSTEP * u + s, 4 * u + p
            dve.wait(t["pair", q], t["BC", u], t.get(("y mm", m - NH)), t["staging"])
            t["mult", m] = dve.run(lambda e: e.tensor_tensor(
                hs[:, m % NH, :].rearrange("p (r t) -> p r t", r=RH),
                du_rep[:, q % NP, jj, :].unsqueeze(1).broadcast_to([P, RH, L]),
                B_rep[:, u % 2, RH * rh:RH * rh + RH, :], ALU.mult))
            t["mult", u, s] = t["mult", m]
            t["du read", q] = t["mult", m]

        def scan(u, s):
            m, d, n = NSTEP * u + s, u % 2, RH * L
            dve.wait(t["mult", m], t["decay", m])
            a = dA[:, m % NA, 0:n] if d == 0 else dA[:, m % NA, 1:n + 1][:, ::-1]
            b = hs[:, m % NH, :] if d == 0 else hs[:, m % NH, :][:, ::-1]
            t["scan", m] = dve.run(lambda e: e.tensor_tensor_scan(b, a, b, 0.0, ALU.mult, ALU.add))
            t["pair used", 4 * u + s // 4] = t["scan", m]

        def times_C(u, s):
            p, rh, jj = place(s)
            m = NSTEP * u + s
            pool.wait(t["scan", m], t["BC", u])
            t["C mult", m] = pool.run(lambda e: e.tensor_tensor(
                hs[:, m % NH, :], hs[:, m % NH, :],
                C_rep[:, u % 2, RH * rh:RH * rh + RH, :].rearrange("p r t -> p (r t)"), ALU.mult))
            t["C mult", u, s] = t["C mult", m]

        def skip_mm(u, h):
            i = 2 * u + h
            pe.wait(t["xi", u, h], t["diag"], t.get(("gated", i - 2)))
            t["D mm", u] = pe.run(lambda e: e.matmul(Y[i % 2][:, :], diag_D[:, u % 2, h, :], xi[:, u % 2, h, :],
                                                     start=True, stop=False, skip_group_check=True))

        def sum_states(u, s):
            p, rh, jj = place(s)
            m, h = NSTEP * u + s, (2 * p) // 4
            pe.wait(t["C mult", m - 1], t["C mult", m])
            for r in range(RH):
                for w in range(2):
                    c = (2 * p + w) % 4
                    i = pe.run(lambda e, r=r, w=w, c=c: e.matmul(
                        Y[h][c * DD:(c + 1) * DD, :], sel, hs[:, (m - 1 + w) % NH, r * L:(r + 1) * L],
                        start=False, stop=(rh == 1 and r == RH - 1), skip_group_check=True),
                        signal=(r == RH - 1 and w == 1))
            t["y mm", m] = t["y mm", m - 1] = i

        def gate(u, h):
            m = NSTEP * u + 8 * h + 7
            dve.wait(t["y mm", m], t["zs", u, h], t.get(("out mm", u // 2 - 1)))
            t["gated", 2 * u + h] = dve.run(lambda e: e.tensor_tensor(
                yg[:, u % 2, h, :], Y[h][:, :], zs[:, u % 2, h, :], ALU.mult))

        def base_load(b):
            sp.wait(t["base stored", b], t.get("attn stored"))
            t["base in"] = dma(base_in[:, :, :], by_batch(base_d, b), "basein")

        def out_mm(b):
            pe.wait(t["gated", 4 * b + 1], t["gated", 4 * b + 3], t["w_out"], t["MB free"])
            for k in range(KB):
                for i in range(4):
                    m = pe.run(lambda e, k=k, i=i: e.matmul(
                        MB[:, k * H:(k + 1) * H], yg[:, i // 2, i % 2, k * P:(k + 1) * P],
                        w_out[:, i // 2, i % 2, :], start=(i == 0), stop=(i == 3)), signal=(k == KB - 1 and i == 3))
            t["out mm", b] = m

        def out_add(b):
            dve.wait(t["out mm", b], t["base in"])
            m = dve.run(lambda e: e.tensor_tensor(base_in[:, :, :].rearrange("p k h -> p (k h)"), MB[:, :],
                                                  base_in[:, :, :].rearrange("p k h -> p (k h)"), ALU.add))
            t["MB free"] = m
            sp.wait(m)
            t["attn stored"] = t["attn stored", b] = dma(by_batch(attn_d, b), base_in[:, :, :], "attnout")

        def scratch(i, n=NBLK * E):
            return gu_w[:, i // 3, :, :].rearrange("p a b -> p (a b)")[:, (i % 3) * 256:(i % 3) * 256 + n]

        def clear_sorted():
            sp.wait(t["sorted0"])
            flat = sorted_d.rearrange("(n p) h -> p n h", p=P)
            for n in range(0, NTILE, KB):
                w = min(KB, NTILE - n)
                t["sorted clear"] = dma(flat[:, n:n + w, :],
                                         act_f[:, :, :].rearrange("p a c -> p (a c)")[:, 0:w * H].rearrange(
                                             "p (n h) -> p n h", h=H), "clear")

        def route():
            one, val, pref, cnt, cum, tmp = (scratch(i) for i in range(6))
            ke = "p (k e) -> p k e"
            iota = cst[:, C_IOTA:C_IOTA + E].unsqueeze(1).broadcast_to([P, NBLK, E])
            best, low = small[:, 0:32], small[:, 32:64]

            def step(fn, *marks):
                dve.wait(*marks)
                m = dve.run(fn)
                dve.wait(m)
                return m

            step(lambda e: e.tensor_reduce(best, logits[:, :, :], AX_X, ALU.max), t["logits"], t["cst"])
            step(lambda e: e.tensor_tensor(val.rearrange(ke, e=E), logits[:, :, :],
                                           best.unsqueeze(2).broadcast_to([P, NBLK, E]), ALU.is_ge))
            step(lambda e: e.scalar_tensor_tensor(val.rearrange(ke, e=E), val.rearrange(ke, e=E), -float(E), iota,
                                                  ALU.mult, ALU.add))
            step(lambda e: e.tensor_reduce(low, val.rearrange(ke, e=E), AX_X, ALU.min))
            m = step(lambda e: e.tensor_tensor(one.rearrange("p (e k) -> p k e", e=E), val.rearrange(ke, e=E),
                                               low.unsqueeze(2).broadcast_to([P, NBLK, E]), ALU.is_equal))
            pe.wait(m, t["ones"], t["TB free"])
            pe.run(lambda e: e.matmul(TB[:, 0:256], tri, one, start=True, stop=True), signal=False)
            m = pe.run(lambda e: e.matmul(TB[:, 256:512], ones[:, :], one, start=True, stop=True))
            step(lambda e: e.tensor_copy(cnt, TB[:, 256:512]), m)
            t["TB free"] = step(lambda e: e.tensor_copy(pref, TB[:, 0:256]))
            step(lambda e: e.tensor_tensor_scan(cum, cst[:, C_NOTFIRST:C_NOTFIRST + 256], cnt, 0.0,
                                                ALU.mult, ALU.add))
            step(lambda e: e.tensor_tensor(pref, pref, cum, ALU.add))
            step(lambda e: e.tensor_tensor(pref, pref, cnt, ALU.subtract))
            total = cum.rearrange("p (e k) -> p e k", e=E)[:, :, NBLK - 1:NBLK].broadcast_to([P, E, NBLK])
            thr = cst[:, C_THR:C_THR + NBLK].unsqueeze(1).broadcast_to([P, E, NBLK])
            step(lambda e: e.tensor_tensor(tmp.rearrange("p (e k) -> p e k", e=E), total, thr, ALU.is_gt))
            ntile, end, first = small[:, 0:E], small[:, E:2 * E], small[:, 2 * E:3 * E]
            step(lambda e: e.tensor_reduce(ntile, tmp.rearrange("p (e k) -> p e k", e=E), AX_X, ALU.add))
            step(lambda e: e.tensor_tensor_scan(end, ones[:, 0:E], ntile, 0.0, ALU.mult, ALU.add), t["ones"])
            step(lambda e: e.tensor_tensor(first, end, ntile, ALU.subtract))
            step(lambda e: e.scalar_tensor_tensor(
                pref.rearrange("p (e k) -> p e k", e=E), first.unsqueeze(2).broadcast_to([P, E, NBLK]), float(P),
                pref.rearrange("p (e k) -> p e k", e=E), ALU.mult, ALU.add))
            step(lambda e: e.tensor_tensor(pref, pref, one, ALU.mult))
            step(lambda e: e.tensor_reduce(low, pref.rearrange("p (e k) -> p k e", e=E), AX_X, ALU.add))
            t["pos"] = step(lambda e: e.tensor_copy(pos_u[:, :], low))
            te = scratch(6, NTILE * E)
            step(lambda e: e.tensor_tensor(
                te.rearrange("p (n e) -> p n e", e=E), end.unsqueeze(1).broadcast_to([P, NTILE, E]),
                cst[:, C_TILE:C_TILE + NTILE].unsqueeze(2).broadcast_to([P, NTILE, E]), ALU.is_le))
            step(lambda e: e.tensor_reduce(tmp[:, 0:NTILE], te.rearrange("p (n e) -> p n e", e=E), AX_X, ALU.add))
            t["tile expert"] = step(lambda e: e.tensor_scalar(ej_i[:, :], tmp[:, 0:NTILE], float(E - 1), None,
                                                              ALU.min))

        def scatter(c):
            sp.wait(t["xn stored"], t.get(("scattered", c - 2)))
            src = attn_in[:, c % 2, :, :]
            got = dma(src, by_batch(xn_d, c), "regather", c % 2)
            pool.wait(got, t["pos"], t["sorted clear"])
            for k in range(KB):
                if ("scatter", c % 2) not in fl:
                    fl["scatter", c % 2] = flow(f"dma_scatter{c % 2}")
                t["scattered", c] = pool.run(lambda e, k=k: e.indirect_dma_start(
                    out=sorted_d, out_offset=bass.IndirectOffsetOnAxis(
                        ap=pos_u[:, c * KB + k:c * KB + k + 1], axis=0),
                    in_=src[:, k, :], in_offset=None), flow=fl["scatter", c % 2], by=16)

        def expert_load(n):
            w = n % NW
            sp.wait(t["scattered", NB - 2], t["scattered", NB - 1], t["tile expert"], t.get(("down mm", n - NW)),
                    t.get(("turn xs", n - 2)))
            t["xs", n] = dma(xs[:, n % 2, :], sorted_d[n * P:(n + 1) * P, :], "xs", n % 2)

            def load(e, dst, src):
                ex = e.value_load(ej_i[0:1, n:n + 1], min_val=0, max_val=E - 1)
                return e.dma_start(dst, src[bass.ds(ex, 1)].rearrange("a p c -> p (a c)"))

            for dst, src in ((gu_w[:, w, :, :].rearrange("p a c -> p (a c)"), gate_up),
                             (dn_w[:, w, :, :].rearrange("p a c -> p (a c)"), down)):
                key = f"dma_experts{w}"
                if key not in fl:
                    fl[key] = flow(key)
                t["weights", n] = sp.run(lambda e, dst=dst, src=src: load(e, dst, src), flow=fl[key], by=16)

        def expert_turn(n):
            pe.wait(t["xs", n], t["TB free"])
            t["turn xs", n] = pe.run(lambda e: e.transpose(TB[:, 0:P], xs[:, n % 2, :], ident))

        def expert_xT(n):
            act.wait(t["turn xs", n], t.get(("up mm", n - 2)))
            t["xsT", n] = act.run(lambda e: e.copy(xsT[:, n % 2, :], TB[:, 0:P]))
            t["TB free"] = t["xsT", n]

        def expert_up(n):
            w = n % NW
            pe.wait(t["xsT", n], t["weights", n], t.get(("acted", n - 1)))
            for a, dst in ((0, GB), (1, UB)):
                for c in range(NCH):
                    m = pe.run(lambda e, a=a, c=c, dst=dst: e.matmul(
                        dst[:, c * P:(c + 1) * P], gu_w[:, w, a, c * P:(c + 1) * P], xsT[:, n % 2, :],
                        start=True, stop=True), signal=c == NCH - 1)
                if a == 0:
                    t["gate mm", n] = m
            t["up mm", n] = m

        def expert_tanh(n):
            act.wait(t["gate mm", n], t.get(("acted", n - 2)))
            t["th_f", n] = act.run(lambda e: e.activation(th_f[:, n % 2, :], GB[:, 0:IFP], ACT.Tanh, scale=0.5))

        def expert_act(n):
            dve.wait(t["th_f", n], t.get(("down mm", n - 2)), t["sorted clear"])
            m = dve.run(lambda e: e.scalar_tensor_tensor(th_f[:, n % 2, :], th_f[:, n % 2, :], 1.0, GB[:, 0:IFP],
                                                         ALU.add, ALU.mult))
            dve.wait(m, t["up mm", n])
            t["acted", n] = dve.run(lambda e: e.scalar_tensor_tensor(
                act_f[:, n % 2, :], th_f[:, n % 2, :], 0.5, UB[:, 0:IFP], ALU.mult, ALU.mult))

        def expert_down(n):
            w = n % NW
            pe.wait(t["acted", n], t["TB free"])
            for c in range(NCH):
                m = pe.run(lambda e, c=c: e.matmul(TB[:, 0:H], act_f[:, n % 2, c * P:(c + 1) * P], dn_w[:, w, c, :],
                                                   start=(c == 0), stop=(c == NCH - 1)), signal=c == NCH - 1)
            t["down mm", n] = m

        def expert_out(n):
            act.wait(t["down mm", n], t.get(("ys stored", n - 2)))
            t["TB free"] = act.run(lambda e: e.copy(ys[:, n % 2, :], TB[:, 0:H]))
            sp.wait(t["TB free"])
            t["ys stored", n] = dma(ffn_d[n * P:(n + 1) * P, :], ys[:, n % 2, :], "ysout", n % 2)

        def gather(b):
            k2 = b % 2
            pool.wait(t["ys stored", NTILE - 2], t["ys stored", NTILE - 1], t.get(("out stored", b - 2)),
                      t["xt free"], t["xn stored"], t["xn read"])
            if ("gather", k2) not in fl:
                fl["gather", k2] = flow(f"dma_gather{k2}")
            for k in range(KB):
                t["gathered", b] = pool.run(lambda e, k=k: e.indirect_dma_start(
                    out=fin[k2][:, k, :], out_offset=None, in_=ffn_d,
                    in_offset=bass.IndirectOffsetOnAxis(ap=pos_u[:, b * KB + k:b * KB + k + 1], axis=0)),
                    flow=fl["gather", k2], by=16)

        def final_load(b):
            k2 = b % 2
            sp.wait(t["attn stored", b], t.get(("out stored", b - 2)), t["scattered", NB - 2 + k2])
            t["attn in", b] = dma(attn_in[:, k2, :, :], by_batch(attn_d, b), "attnin", k2)

        def final(b):
            k2 = b % 2
            dve.wait(t["attn in", b], t["gathered", b])
            m = dve.run(lambda e: e.tensor_tensor(fin[k2][:, :, :], fin[k2][:, :, :], attn_in[:, k2, :, :], ALU.add))
            sp.wait(m)
            t["out stored", b] = dma(by_batch(out, b), fin[k2][:, :, :], "out", k2)

        later = {}

        def at(step, fn, *a):
            later.setdefault(step, []).append((fn, a))

        def front(v, s0=None):
            plan = [(-5, batch_turn, v // 2)] if v % 2 == 0 else []
            plan += [(-4, in_proj, v, 0), (-3, in_proj, v, 1), (-2, xi_act, v, 0), (-1, xi_act, v, 1),
                     (0, z_proj, v, 0), (1, xi_mul, v, 0), (1, xi_mul, v, 1), (1, z_proj, v, 1),
                     (2, z_act, v, 0), (3, z_act, v, 1), (2, x_proj, v), (4, z_mul, v, 0), (4, z_mul, v, 1),
                     (4, dbc_out, v), (5, dt_proj, v), (5, BC_load, v), (6, softplus_max, v),
                     (7, softplus_log, v), (8, delta_out, v), (10, pair_load, v, 0), (12, pair_load, v, 1)]
            for k, fn, *a in sorted(plan, key=lambda x: x[0]):
                if s0 is None:
                    fn(*a)
                else:
                    at(max(0, s0 + k), fn, *a)

        ln_load(0)
        ln_first(0)
        ln_second(0)
        ln_third(0)
        batch_load(0)
        front(0)
        clear_sorted()
        for u in range(UNITS):
            s0 = NSTEP * u
            at(s0, pair_load, u, 2)
            at(s0 + 4, pair_load, u, 3)
            if u + 1 < UNITS:
                front(u + 1, s0)
                if u % 2 == 0 and u + 2 < UNITS:
                    at(s0 + 9, batch_load, (u + 2) // 2)
            at(s0 + 10, gate, u, 0)
            at(s0 + NSTEP + 2, gate, u, 1)
            if u % 2 == 1:
                at(s0 + NSTEP - 2, base_load, u // 2)
                at(s0 + NSTEP + 7, out_mm, u // 2)
                at(s0 + NSTEP + 9, out_add, u // 2)
        for c in range(1, NB):
            s0 = 8 * (c - 1)
            at(s0, ln_load, c)
            at(s0 + 2, ln_first, c)
            at(s0 + 4, ln_second, c)
            at(s0 + 7, ln_third, c)
        r0 = 8 * (NB - 1) + 2
        at(r0, route)
        for c in range(NB):
            at(r0 + 2 + 2 * c, scatter, c)
        f0, gap = r0 + 24, 3
        for n in range(NTILE):
            s0 = f0 + gap * n
            for k, fn in ((0, expert_load), (3, expert_turn), (4, expert_xT), (5, expert_up), (6, expert_tanh),
                          (7, expert_act), (8, expert_down), (9, expert_out)):
                at(s0 + k, fn, n)
        g0 = f0 + gap * NTILE + 10
        last = UNITS * NSTEP
        for b in range(NB):
            s0 = max(g0 + 4 * b, NSTEP * (2 * b + 2) + 9)
            at(s0, gather, b)
            at(s0, final_load, b)
            at(s0 + 3, final, b)
        for m in range(LEAD):
            decay(0, m)
        du_B(0, 0)
        m = 0
        while m < last or any(k >= m for k in later):
            if m + LEAD < last:
                decay(*divmod(m + LEAD, NSTEP))
            for fn, a in later.get(m, ()):
                fn(*a)
            if m < last:
                u, s = divmod(m, NSTEP)
                if s % 8 == 0:
                    skip_mm(u, s // 8)
                if m + 1 < last:
                    du_B(*divmod(m + 1, NSTEP))
                scan(u, s)
                times_C(u, s)
                if s % 2:
                    sum_states(u, s)
            m += 1
        for name, f in list(fl.items()):
            sp.wait((f, f.value))

        block = ctx.enter_context(nc.Block())

        @block.sync
        def _(e):
            sp.play(e)

        @block.tensor
        def _(e):
            pe.play(e)

        @block.scalar
        def _(e):
            act.play(e)

        @block.vector
        def _(e):
            dve.play(e)

        @block.gpsimd
        def _(e):
            pool.play(e)


def shape_constants():
    import numpy as np
    c = np.zeros((P, C_END), np.float32)
    c[:, C_ID:C_ID + P] = np.eye(P)
    c[:, C_TRI:C_TRI + P] = np.triu(np.ones((P, P)), 1)
    c[:, C_SEL:C_SEL + DD] = np.tile(np.eye(DD), (G, 1))
    c[:, C_IOTA:C_IOTA + E] = np.arange(E)
    c[:, C_THR:C_THR + NBLK] = P * np.arange(NBLK)
    c[:, C_NOTFIRST:C_NOTFIRST + E * NBLK] = np.tile(np.arange(NBLK) > 0, E)
    c[:, C_TILE:C_TILE + NTILE] = np.arange(NTILE)
    return c


def kernel(**inputs):
    import numpy as np
    import concourse.bacc as bacc
    from concourse.bass_utils import run_bass_kernel_spmd

    a = {k: np.asarray(v) for k, v in inputs.items()}

    def both(name, lay):
        return np.ascontiguousarray(np.stack([lay(a[f"L0_attn_{d}_{name}"]) for d in "fb"]))

    def halves(v):
        return v.reshape(2, P).T

    gate_up = np.zeros((E, P, 2, IFP), np.float32)
    gate_up[:, :, 0, :IF] = a["L0_ffn_gate_w"].transpose(0, 2, 1)
    gate_up[:, :, 1, :IF] = a["L0_ffn_up_w"].transpose(0, 2, 1)
    down = np.zeros((E, IFP, H), np.float32)
    down[:, :IF] = a["L0_ffn_down_w"].transpose(0, 2, 1)
    arrays = {
        "x": a["L0_attn_x"].reshape(NBLK * P, H),
        "in_wT": both("in_w", lambda w: w.T),
        "conv_wT": both("conv_w", lambda w: w.T),
        "conv_b": both("conv_b", halves),
        "x_wT": both("x_w", lambda w: w.T.reshape(2, P, NDBC).transpose(1, 0, 2)),
        "dt_wT": both("dt_w", lambda w: w.T),
        "dt_b": both("dt_b", halves),
        "A_log": both("A_log", lambda w: w.reshape(J, DD, G, R).transpose(2, 1, 0, 3).reshape(P, J, R)),
        "Dp": both("D", halves),
        "out_w": both("out_w", lambda w: w),
        "comb_wT": a["L0_attn_combine_w"].T.reshape(2, P, H).transpose(1, 0, 2),
        "comb_b": a["L0_attn_combine_b"].reshape(1, H),
        "ln_g": a["L0_attn_ln_g"].reshape(P, 1),
        "ln_b": a["L0_attn_ln_b"].reshape(P, 1),
        "router_wT": a["L0_ffn_router_w"].T,
        "gate_up": gate_up.reshape(E, P, 2 * IFP),
        "down": down.reshape(E, NCH, P, H).transpose(0, 2, 1, 3).reshape(E, P, NCH * H),
        "consts": shape_constants(),
    }
    nc = bacc.Bacc("TRN2", target_bir_lowering=False, num_devices=1)
    fed, args = {}, []
    for name, v in arrays.items():
        v = np.ascontiguousarray(v)
        fed["in_" + name] = v
        args.append(nc.dram_tensor("in_" + name, v.shape, mybir.dt.from_np(v.dtype), kind="ExternalInput").ap())
    out = nc.dram_tensor("out_0", (NBLK * P, H), F32, kind="ExternalOutput").ap()
    mamba_moe_kernel(nc, *args, out)
    r = run_bass_kernel_spmd(nc, [fed], core_ids=[0])
    return r.results[0]["out_0"].reshape(NB, L, H)
```

```python
from contextlib import ExitStack

import concourse.bass as bass
from concourse import mybir

F32 = mybir.dt.float32
I32 = mybir.dt.int32
U32 = mybir.dt.uint32
ALU = mybir.AluOpType
ACT = mybir.ActivationFunctionType
AX_X = mybir.AxisListType.X

P = 128
NB, L, H = 8, 512, 128
KB = L // P
NBLK = NB * KB
DI, DS, DR, NTAP = 256, 16, 8, 4
NDBC = DR + 2 * DS
G, DD = 4, 32
R = DS // G
J = DI // DD
RH = 2
NSTEP = J * R // RH
UNITS = 2 * NB
E, IF, IFP = 8, 352, 384
NCH = IFP // P
NTILE = NBLK + E - 1
EPS = 1e-5

C_ID, C_TRI, C_SEL, C_IOTA, C_THR, C_NOTFIRST, C_TILE = 0, 128, 256, 288, 296, 328, 584
C_END = C_TILE + NTILE
NCOL = 14


class Flow:

    def __init__(self, sem):
        self.sem, self.value = sem, 0


class Queue:

    def __init__(self, own):
        self.ops, self.own, self.met = [], own, {}

    def wait(self, *marks):
        for mark in marks:
            if mark is None:
                continue
            flow, value = mark
            if self.met.get(id(flow), 0) >= value:
                continue
            self.met[id(flow)] = value
            self.ops.append(lambda e, s=flow.sem, v=value: e.wait_ge(s, v))

    def run(self, fn, signal=True, flow=None, by=1):
        if not signal:
            self.ops.append(fn)
            return None
        flow = flow or self.own
        flow.value += by
        self.ops.append(lambda e: fn(e).then_inc(flow.sem, by))
        return flow, flow.value

    def play(self, e):
        for op in self.ops:
            op(e)


def mamba_moe_kernel(nc, x, in_wT, conv_wT, x_wT, dt_wT, A_log, out_w, comb_wT, comb_b,
                     col_vectors, router_wT, gate_up, down, consts, out):
    ctx = ExitStack()
    with ctx:
        def sb(name, shape, dt=F32):
            return ctx.enter_context(nc.sbuf_tensor(name, shape, dt))

        def flow(name):
            return Flow(ctx.enter_context(nc.semaphore(name)))

        def dram(name, shape, dt=F32):
            return nc.dram_tensor(name, shape, dt, kind="Internal").ap()

        xn_d = dram("xn_scratch", (NBLK * P, H))
        xn2_d = dram("xn2_scratch", (NBLK * P, H))
        base_d = dram("base_scratch", (NBLK * P, H))
        attn_d = dram("attn_scratch", (NBLK * P, H))
        sorted_d = dram("sorted_tokens", (NTILE * P, H))
        ffn_d = dram("sorted_ffn", (NTILE * P, H))
        delta_d = dram("delta_scratch", (2, DD, J, L))
        du_d = dram("du_scratch", (2, DD, J, L))
        dbc_d = dram("dbc_scratch", (2, NDBC, L))

        def by_batch(t, b):
            return t.rearrange("(b k p) h -> b p k h", b=NB, p=P)[b]

        cst = sb("cst", [P, C_END])
        ones = sb("ones", [P, P])
        neg_half = sb("neg_half", [P, KB])
        w_in = sb("w_in", [P, 2, NTAP + 1, DI])
        w_x = sb("w_x", [P, 2, 2, NDBC])
        w_dt = sb("w_dt", [DR, 2, DI])
        diag_D = sb("diag_D", [P, 2, 2, P])
        w_out = sb("w_out", [P, 2, 2, H])
        cols = sb("cols", [P, 16])
        A_sb = sb("A_sb", [P, 2, J, R])
        rw = sb("rw", [P, E])
        comb_bias = sb("comb_bias", [1, H])
        xt = sb("xt", [P, KB, H])
        xn = sb("xn", [P, KB, H])
        xn2 = sb("xn2", [P, KB, H])
        stats = sb("stats", [P, KB, 6])
        moments = sb("moments", [P, KB, 2])
        rstd = sb("rstd", [P, KB])
        rstd2 = sb("rstd2", [P, KB])
        xnT = sb("xnT", [P, L])
        xn2_in = sb("xn2_in", [P, KB, H])
        xpad = sb("xpad", [P, 2, L + 6])
        xi = sb("xi", [P, 2, 2, L])
        tmpA = sb("tmpA", [P, 2, L])
        tmpB = sb("tmpB", [P, 2, L])
        du = tmpB
        zs = sb("zs", [P, 2, 2, L])
        dbc = sb("dbc", [NDBC, L])
        NP = 3
        delta_rep = sb("delta_rep", [P, NP, 2, L])
        du_rep = sb("du_rep", [P, NP, 2, L])
        B_rep = sb("B_rep", [P, 2, R, L])
        C_rep = sb("C_rep", [P, 2, R, L])
        NA, NH, LEAD = 4, 8, 3
        SUM_LAG = 1
        LN_STEPS = 7
        dA = sb("dA", [P, NA, RH * L + 1])
        hs = sb("hs", [P, NH, RH * L])
        yg = sb("yg", [P, 2, 2, L])
        base_in = sb("base_in", [P, KB, H])
        NW = 3
        gu_w = sb("gu_w", [P, NW, 2, IFP])
        dn_w = sb("dn_w", [P, NW, NCH, H])
        xs = sb("xs", [P, 2, H])
        xsT = sb("xsT", [P, 2, P])
        th_f = sb("th_f", [P, 2, IFP])
        act_f = sb("act_f", [P, 2, IFP])
        ys = sb("ys", [P, 2, H])
        fin = (xt, xn)
        attn_in = sb("attn_in", [P, 2, KB, H])
        logits = sb("logits", [P, NBLK, E])
        pos_u = sb("pos_u", [P, NBLK], U32)
        ej_i = sb("ej_i", [P, NTILE], I32)
        small = sb("small", [P, 64])

        def bank(name):
            return ctx.enter_context(nc.psum_tensor(name, [P, 512], F32))

        Y = [bank("y0"), bank("y1")]
        FB = [bank("front0"), bank("front1")]
        MB = bank("mixed")
        GB, UB, TB = bank("gate"), bank("up"), bank("turn")

        pe, act, dve, pool, sp = (Queue(flow("done_" + n)) for n in ("pe", "act", "dve", "pool", "sp"))
        fl = {}

        def dma(dst, src, name, k=0, q=None):
            key = f"dma_{name}{k}"
            if key not in fl:
                fl[key] = flow(key)
            return (q or sp).run(lambda e: e.dma_start(dst, src), flow=fl[key], by=16)

        t = {}

        ident = cst[:, C_ID:C_ID + P]
        tri = cst[:, C_TRI:C_TRI + P]
        sel = cst[:, C_SEL:C_SEL + DD]

        cwb = delta_rep[:, :, :, :].rearrange("p a b c -> p (a b c)")[:, 0:2 * NTAP * DI].rearrange(
            "p (d k c) -> p d k c", d=2, k=NTAP)
        inw_t = du_rep[:, :, :, :].rearrange("p a b c -> p (a b c)")[:, 0:2 * 2 * DI].rearrange(
            "p (d c) -> p d c", d=2)
        outw_t = hs[:, 0, 0:2 * DI].rearrange("p (d c) -> p d c", d=2)
        combw_t = hs[:, 1, 0:2 * H].rearrange("p (d o) -> p d o", d=2)
        t["xt"] = dma(xt[:, :, :], by_batch(x, 0), "xt")
        dma(cwb.rearrange("p d k c -> p (d k c)"), conv_wT.unsqueeze(0).broadcast_to([P, 2 * NTAP * DI]), "wfront")
        dma(inw_t, in_wT, "wfront")
        dma(cols[:, 0:NCOL], col_vectors, "wfront")
        t["cst"] = front_weights_in = dma(cst[:, :], consts, "wfront")
        dma(w_x[:, :, :, :], x_wT, "w", q=act)
        dma(w_dt[:, :, :], dt_wT, "w", q=act)
        dma(A_sb[:, :, :, :], A_log, "w", q=act)
        dma(outw_t, out_w, "w", q=act)
        dma(combw_t, comb_wT, "w", q=act)
        dma(rw[:, :], router_wT, "w", q=act)
        weights_in = dma(comb_bias[:, :], comb_b, "w", q=act)

        def conv_bias(d, h):
            return cols[:, 2 * d + h:2 * d + h + 1]

        def dt_bias(d, h):
            return cols[:, 4 + 2 * d + h:5 + 2 * d + h]

        t["ones"] = dve.run(lambda e: e.memset(ones[:, :], 1.0))
        t["pow"] = dve.run(lambda e: e.memset(neg_half[:, :], -0.5))
        dve.run(lambda e: e.memset(xpad[:, :, 0:NTAP - 1], 0.0), signal=False)
        t["xpad0"] = dve.run(lambda e: e.memset(xpad[:, :, L + NTAP - 1:], 0.0))
        t["dA0"] = dve.run(lambda e: e.memset(dA[:, :, 0:RH * L + 1:L], 0.0))
        t["sorted0"] = pool.run(lambda e: e.memset(act_f[:, :, :], 0.0))

        def prepare_front():
            dve.wait(front_weights_in)
            for d in range(2):
                t["w_in"] = dve.run(lambda e, d=d: e.scalar_tensor_tensor(
                    w_in[:, d, 0:NTAP, :], inw_t[:, d, 0:DI].unsqueeze(1).broadcast_to([P, NTAP, DI]), 0.5,
                    cwb[:, d, :, :], ALU.mult, ALU.mult))
                t["w_in"] = dve.run(lambda e, d=d: e.tensor_scalar(
                    w_in[:, d, NTAP, :], inw_t[:, d, DI:2 * DI], 0.5, None, ALU.mult))
            t["conv_bias"] = dve.run(lambda e: e.tensor_scalar(cols[:, 0:4], cols[:, 0:4], 0.5, None, ALU.mult))

        def prepare_A():
            act.wait(weights_in)
            m = act.run(lambda e: e.activation(A_sb[:, :, :, :], A_sb[:, :, :, :], ACT.Exp))
            act.wait(m)
            t["A"] = act.run(lambda e: e.mul(A_sb[:, :, :, :], A_sb[:, :, :, :], -1.0))

        def prepare_rest():
            dve.wait(front_weights_in)
            for d in range(2):
                for h in range(2):
                    t["diag"] = dve.run(lambda e, d=d, h=h: e.tensor_scalar(
                        diag_D[:, d, h, :], ident, cols[:, 8 + 2 * d + h:9 + 2 * d + h], None, ALU.mult))
            pe.wait(weights_in, t["MB free"])
            for d in range(2):
                for h in range(2):
                    m = pe.run(lambda e, d=d, h=h: e.matmul(
                        MB[:, (2 * d + h) * H:(2 * d + h + 1) * H], outw_t[:, d, h * P:(h + 1) * P],
                        combw_t[:, d, :], start=True, stop=True))
            dve.wait(m)
            t["w_out"] = dve.run(lambda e: e.tensor_copy(
                w_out[:, :, :, :].rearrange("p d h o -> p (d h o)"), MB[:, :]))
            t["MB free"] = t["staging"] = t["w_out"]

        def moments_of(src, mark, r):
            dve.wait(mark)
            for k in range(KB):
                s = dve.run(lambda e, k=k: e.bn_stats(stats[:, k, :], src[:, k, :]))
            dve.wait(s)
            for k in range(KB):
                m = dve.run(lambda e, k=k: e.bn_aggr(moments[:, k, :], stats[:, k, :]))
            pool.wait(m, t["pow"])
            v = pool.run(lambda e: e.tensor_scalar(r[:, :], moments[:, :, 1], EPS, None, ALU.add))
            pool.wait(v)
            return pool.run(lambda e: e.tensor_tensor(r[:, :], r[:, :], neg_half[:, :], ALU.pow))

        def normalize(dst, src, r):
            for k in range(KB):
                m = dve.run(lambda e, k=k: e.tensor_scalar(
                    dst[:, k, :], src[:, k, :], moments[:, k, 0:1], r[:, k:k + 1], ALU.subtract, ALU.mult))
            return m

        def ln_load(c):
            sp.wait(t.get("xt free"))
            t["xt"] = dma(xt[:, :, :], by_batch(x, c), "xt")

        def ln_first(c):
            t["rstd"] = moments_of(xt, t["xt"], rstd)

        def ln_second(c):
            dve.wait(t["rstd"], t.get("xn stored"), t.get("xn read"))
            t["xn"] = normalize(xn, xt, rstd)
            t["rstd2"] = moments_of(xn, t["xn"], rstd2)
            pool.wait(t["xn"])
            t["base"] = pool.run(lambda e: e.tensor_tensor(xt[:, :, :], xt[:, :, :], xn[:, :, :], ALU.add))
            sp.wait(t["xn"])
            t["xn stored"] = dma(by_batch(xn_d, c), xn[:, :, :], "xnout")
            sp.wait(t["base"])
            t["xt free"] = dma(by_batch(base_d, c), xt[:, :, :], "baseout")
            t["base stored", c] = t["xt free"]
            pe.wait(t["xn"], t["cst"], t.get("TB free"))
            for k in range(KB):
                m = pe.run(lambda e, k=k: e.transpose(TB[:, k * P:(k + 1) * P], xn[:, k, :], ident))
            t["xn read"] = m
            act.wait(m, t.get("logits mm"))
            t["xnT"] = act.run(lambda e: e.copy(xnT[:, :], TB[:, :]))

        def ln_third(c):
            dve.wait(t["rstd2"], t.get("xn2 stored"), t.get("xn2 turned"))
            m = normalize(xn2, xn, rstd2)
            t["xn read"] = m
            sp.wait(m)
            t["xn2 stored"] = dma(by_batch(xn2_d, c), xn2[:, :, :], "xn2out")
            t["xn2 in dram", c] = t["xn2 stored"]
            t["xn2"] = m
            pe.wait(t["xnT"], weights_in)
            for k in range(KB):
                m = pe.run(lambda e, k=k: e.matmul(TB[:, k * E:(k + 1) * E], xnT[:, k * P:(k + 1) * P], rw[:, :],
                                                   start=True, stop=True))
            t["logits mm"] = m
            act.wait(m)
            t["TB free"] = act.run(lambda e: e.copy(
                logits[:, c * KB:(c + 1) * KB, :].rearrange("p k e -> p (k e)"), TB[:, 0:KB * E]))
            t["logits"] = t["TB free"]

        def batch_load(b):
            sp.wait(t["xn2 in dram", b], t.get("xn2_in free"))
            t["xn2_in"] = dma(xn2_in[:, :, :], by_batch(xn2_d, b), "xn2in")

        def batch_turn(b):
            src = xn2_in if b else xn2
            pe.wait(t["xn2_in"] if b else t["xn2"], t["cst"], t.get(("FB free", 0)))
            for k in range(KB):
                m = pe.run(lambda e, k=k: e.transpose(FB[0][:, k * P:(k + 1) * P], src[:, k, :], ident))
            t["xn2_in free" if b else "xn2 turned"] = m
            act.wait(m, t["xpad0"], front_weights_in, t.get(("in proj", 2 * b - 3)))
            t["xpad", b] = act.run(lambda e: e.activation(
                xpad[:, b % 2, 3:3 + L], FB[0][:, :], ACT.Identity, scale=cols[:, 12:13], bias=cols[:, 13:14]))
            t["FB free", 0] = t["xpad", b]

        def in_proj(v, h, part=None):
            b, d = divmod(v, 2)
            pe.wait(t["xpad", b], t["w_in"], t.get(("FB free", 1 - h)))
            for k in range(NTAP) if part is None else range(2 * part, 2 * part + 2):
                at = k if d == 0 else 2 * (NTAP - 1) - k
                m = pe.run(lambda e, k=k, at=at: e.matmul(
                    FB[1 - h][:, :], w_in[:, d, k, h * P:(h + 1) * P], xpad[:, b % 2, at:at + L],
                    start=(k == 0), stop=(k == NTAP - 1)), signal=k == NTAP - 1)
            t["in", v, h] = m

        def z_proj(v, h):
            b, d = divmod(v, 2)
            pe.wait(t["FB free", 1 - h])
            t["z", v, h] = pe.run(lambda e: e.matmul(
                FB[1 - h][:, :], w_in[:, d, NTAP, h * P:(h + 1) * P], xpad[:, b % 2, 3:3 + L],
                start=True, stop=True))
            t["in proj", v] = t["z", v, h]

        def xi_act(v, h):
            act.wait(t["in", v, h], t["conv_bias"], t.get(("du stored", v - 1, h)))
            act.run(lambda e: e.activation(tmpA[:, h, :], FB[1 - h][:, :], ACT.Identity,
                                           bias=conv_bias(v % 2, h)), signal=False)
            t["th", v, h] = act.run(lambda e: e.activation(tmpB[:, h, :], FB[1 - h][:, :], ACT.Tanh,
                                                           bias=conv_bias(v % 2, h)))
            t["FB free", 1 - h] = t["th", v, h]

        def xi_mul(v, h):
            dve.wait(t["th", v, h], t.get(("D mm", v - 2)), t.get(("du made", v - 2)))
            t["xi", v, h] = dve.run(lambda e: e.scalar_tensor_tensor(
                xi[:, v % 2, h, :], tmpB[:, h, :], 1.0, tmpA[:, h, :], ALU.add, ALU.mult))

        def z_act(v, h):
            act.wait(t["z", v, h], t["xi", v, h])
            t["thz", v, h] = act.run(lambda e: e.activation(tmpB[:, h, :], FB[1 - h][:, :], ACT.Tanh))

        def z_mul(v, h):
            dve.wait(t["thz", v, h], t.get(("gated", 2 * (v - 2) + h)))
            t["zs", v, h] = dve.run(lambda e: e.scalar_tensor_tensor(
                zs[:, v % 2, h, :], tmpB[:, h, :], 1.0, FB[1 - h][:, :], ALU.add, ALU.mult))
            t["FB free", 1 - h] = t["zs", v, h]

        def x_proj(v):
            d = v % 2
            pe.wait(t["xi", v, 0], t["xi", v, 1], weights_in, t.get("MB free"))
            for h in range(2):
                m = pe.run(lambda e, h=h: e.matmul(MB[0:NDBC, :], w_x[:, d, h, :], xi[:, v % 2, h, :],
                                                   start=(h == 0), stop=(h == 1)), signal=h == 1)
            t["dbc mm"] = m

        def dbc_out(v):
            act.wait(t["dbc mm"], t.get("dbc stored"), t.get(("dt", v - 1, 1)))
            t["dbc"] = act.run(lambda e: e.copy(dbc[:, :], MB[0:NDBC, :]))
            t["MB free"] = t["dbc"]
            sp.wait(t["dbc"], t.get(("BC", v - 2)))
            t["dbc stored"] = dma(dbc_d[v % 2], dbc[:, :], "dbcout")

        def dt_proj(v):
            d = v % 2
            pe.wait(t["dbc"])
            for h in range(2):
                pe.wait(t["FB free", 1 - h])
                t["dt", v, h] = pe.run(lambda e, h=h: e.matmul(
                    FB[1 - h][:, :], w_dt[:, d, h * P:(h + 1) * P], dbc[0:DR, :], start=True, stop=True))

        def softplus(v):
            for h in range(2):
                act.wait(t["dt", v, h], t["xi", v, h], t["zs", v, h])
                act.run(lambda e, h=h: e.activation(tmpA[:, h, :], FB[1 - h][:, :], ACT.Relu,
                                                    bias=dt_bias(v % 2, h)), signal=False)
                m = t["FB free", 1 - h] = act.run(lambda e, h=h: e.activation(
                    tmpB[:, h, :], FB[1 - h][:, :], ACT.Abs, bias=dt_bias(v % 2, h)))
            act.wait(m)
            m = act.run(lambda e: e.activation(tmpB[:, :, :], tmpB[:, :, :], ACT.Exp, scale=-1.0))
            act.wait(m)
            for h in range(2):
                t["log", v, h] = act.run(lambda e, h=h: e.activation(tmpB[:, h, :], tmpB[:, h, :], ACT.Ln, bias=1.0))

        def BC_load(v):
            k = v % 2
            sp.wait(t["dbc stored"], t.get(("mult", v - 2, NSTEP - 1)), t.get(("C mult", v - 2, NSTEP - 1)))
            for dst, row in ((B_rep, DR), (C_rep, DR + DS)):
                t["BC", v] = dma(dst[:, k, :, :].rearrange("p r t -> p (r t)"),
                                 dbc_d[k, row:row + DS, :].rearrange("(g r) t -> g (r t)", g=G)
                                 .unsqueeze(1).broadcast_to([G, DD, R * L]), "bc", k)

        def delta_out(v, eng=None):
            eng, k = eng or pool, v % 2
            for h in range(2):
                eng.wait(t["log", v, h])
                t["delta", v, h] = eng.run(lambda e, h=h: e.tensor_tensor(
                    tmpA[:, h, :], tmpA[:, h, :], tmpB[:, h, :], ALU.add))
                eng.wait(t["delta", v, h], t["xi", v, h])
                t["du made", v] = eng.run(lambda e, h=h: e.tensor_tensor(
                    du[:, h, :], tmpA[:, h, :], xi[:, k, h, :], ALU.mult))
                sp.wait(t["delta", v, h], t.get(("pair", 4 * (v - 2) + 3)))
                dma(delta_d[k].rearrange("e j t -> j e t")[4 * h:4 * h + 4], tmpA[:, h, :], "dout", h)
                sp.wait(t["du made", v])
                t["du stored", v, h] = dma(
                    du_d[k].rearrange("e j t -> j e t")[4 * h:4 * h + 4], du[:, h, :], "dout", h)

        def pair_load(v, p):
            k, q = v % 2, 4 * v + p
            sp.wait(t["du stored", v, p // 2], t.get(("pair used", q - NP)), t["w_in"])
            for dst, src in ((delta_rep, delta_d), (du_rep, du_d)):
                t["pair", q] = dma(dst[:, q % NP, :, :].rearrange("p j t -> p (j t)"),
                                   src[k, :, 2 * p:2 * p + 2, :].rearrange("e j t -> e (j t)")
                                   .unsqueeze(0).broadcast_to([G, DD, 2 * L]), "pair", q % NP)

        def place(s):
            return s // 4, (s // 2) % 2, s % 2

        def decay(u, s):
            p, rh, jj = place(s)
            m, q, d = NSTEP * u + s, 4 * u + p, u % 2
            act.wait(t["pair", q], t["A"], t["dA0"], t.get(("scan", m - NA)))
            src = delta_rep[:, q % NP, jj, 1:L] if d == 0 else delta_rep[:, q % NP, jj, 0:L - 1]
            for r in range(RH):
                i = act.run(lambda e, r=r: e.activation(
                    dA[:, m % NA, r * L + 1:(r + 1) * L], src, ACT.Exp,
                    scale=A_sb[:, d, 2 * p + jj, RH * rh + r:RH * rh + r + 1]), signal=r == RH - 1)
            t["decay", m] = i

        def du_B(u, s):
            p, rh, jj = place(s)
            m, q = NSTEP * u + s, 4 * u + p
            dve.wait(t["pair", q], t["BC", u], t.get(("y mm", m - NH)), t["staging"])
            t["mult", m] = dve.run(lambda e: e.tensor_tensor(
                hs[:, m % NH, :].rearrange("p (r t) -> p r t", r=RH),
                du_rep[:, q % NP, jj, :].unsqueeze(1).broadcast_to([P, RH, L]),
                B_rep[:, u % 2, RH * rh:RH * rh + RH, :], ALU.mult))
            t["mult", u, s] = t["mult", m]
            t["du read", q] = t["mult", m]

        def scan(u, s):
            m, d, n = NSTEP * u + s, u % 2, RH * L
            dve.wait(t["mult", m], t["decay", m])
            a = dA[:, m % NA, 0:n] if d == 0 else dA[:, m % NA, 1:n + 1][:, ::-1]
            b = hs[:, m % NH, :] if d == 0 else hs[:, m % NH, :][:, ::-1]
            t["scan", m] = dve.run(lambda e: e.tensor_tensor_scan(b, a, b, 0.0, ALU.mult, ALU.add))
            t["pair used", 4 * u + s // 4] = t["scan", m]

        def times_C(u, s):
            p, rh, jj = place(s)
            m = NSTEP * u + s
            pool.wait(t["scan", m], t["BC", u])
            t["C mult", m] = pool.run(lambda e: e.tensor_tensor(
                hs[:, m % NH, :], hs[:, m % NH, :],
                C_rep[:, u % 2, RH * rh:RH * rh + RH, :].rearrange("p r t -> p (r t)"), ALU.mult))
            t["C mult", u, s] = t["C mult", m]

        def skip_mm(u, h):
            i = 2 * u + h
            pe.wait(t["xi", u, h], t["diag"], t.get(("gated", i - 2)))
            t["D mm", u] = pe.run(lambda e: e.matmul(Y[i % 2][:, :], diag_D[:, u % 2, h, :], xi[:, u % 2, h, :],
                                                     start=True, stop=False, skip_group_check=True))

        def sum_states(u, s):
            p, rh, jj = place(s)
            m, h = NSTEP * u + s, (2 * p) // 4
            pe.wait(t["C mult", m - 1], t["C mult", m])
            for r in range(RH):
                for w in range(2):
                    c = (2 * p + w) % 4
                    i = pe.run(lambda e, r=r, w=w, c=c: e.matmul(
                        Y[h][c * DD:(c + 1) * DD, :], sel, hs[:, (m - 1 + w) % NH, r * L:(r + 1) * L],
                        start=False, stop=(rh == 1 and r == RH - 1), skip_group_check=True),
                        signal=(r == RH - 1 and w == 1))
            t["y mm", m] = t["y mm", m - 1] = i

        def gate(u, h):
            m = NSTEP * u + 8 * h + 7
            dve.wait(t["y mm", m], t["zs", u, h], t.get(("out mm", u // 2 - 1)))
            t["gated", 2 * u + h] = dve.run(lambda e: e.tensor_tensor(
                yg[:, u % 2, h, :], Y[h][:, :], zs[:, u % 2, h, :], ALU.mult))

        def base_load(b):
            sp.wait(t["base stored", b], t.get("attn stored"))
            t["base in"] = dma(base_in[:, :, :], by_batch(base_d, b), "basein")

        def out_mm(b, k):
            pe.wait(t["gated", 4 * b + 1], t["gated", 4 * b + 3], t["w_out"], t["ones"], t["MB free"])
            for i in range(4):
                pe.run(lambda e, i=i: e.matmul(
                    MB[:, k * H:(k + 1) * H], yg[:, i // 2, i % 2, k * P:(k + 1) * P],
                    w_out[:, i // 2, i % 2, :], start=(i == 0), stop=False), signal=False)
            m = pe.run(lambda e: e.matmul(MB[:, k * H:(k + 1) * H], ones[0:1, :], comb_bias[:, :],
                                          start=False, stop=True))
            t["out mm", b] = m

        def out_add(b):
            dve.wait(t["out mm", b], t["base in"])
            m = dve.run(lambda e: e.tensor_tensor(base_in[:, :, :].rearrange("p k h -> p (k h)"), MB[:, :],
                                                  base_in[:, :, :].rearrange("p k h -> p (k h)"), ALU.add))
            t["MB free"] = m
            sp.wait(m)
            t["attn stored"] = t["attn stored", b] = dma(by_batch(attn_d, b), base_in[:, :, :], "attnout")

        def scratch(i, n=NBLK * E):
            return gu_w[:, i // 3, :, :].rearrange("p a b -> p (a b)")[:, (i % 3) * 256:(i % 3) * 256 + n]

        def clear_sorted():
            sp.wait(t["sorted0"])
            flat = sorted_d.rearrange("(n p) h -> p n h", p=P)
            for n in range(0, NTILE, KB):
                w = min(KB, NTILE - n)
                t["sorted clear"] = dma(flat[:, n:n + w, :],
                                         act_f[:, :, :].rearrange("p a c -> p (a c)")[:, 0:w * H].rearrange(
                                             "p (n h) -> p n h", h=H), "clear")

        def route():
            one, val, pref, cnt, cum, tmp = (scratch(i) for i in range(6))
            ke = "p (k e) -> p k e"
            iota = cst[:, C_IOTA:C_IOTA + E].unsqueeze(1).broadcast_to([P, NBLK, E])
            best, low = small[:, 0:32], small[:, 32:64]

            def step(fn, *marks):
                dve.wait(*marks)
                m = dve.run(fn)
                dve.wait(m)
                return m

            step(lambda e: e.tensor_reduce(best, logits[:, :, :], AX_X, ALU.max), t["logits"], t["cst"])
            step(lambda e: e.tensor_tensor(val.rearrange(ke, e=E), logits[:, :, :],
                                           best.unsqueeze(2).broadcast_to([P, NBLK, E]), ALU.is_ge))
            step(lambda e: e.scalar_tensor_tensor(val.rearrange(ke, e=E), val.rearrange(ke, e=E), -float(E), iota,
                                                  ALU.mult, ALU.add))
            step(lambda e: e.tensor_reduce(low, val.rearrange(ke, e=E), AX_X, ALU.min))
            m = step(lambda e: e.tensor_tensor(one.rearrange("p (e k) -> p k e", e=E), val.rearrange(ke, e=E),
                                               low.unsqueeze(2).broadcast_to([P, NBLK, E]), ALU.is_equal))
            pe.wait(m, t["ones"], t["TB free"])
            pe.run(lambda e: e.matmul(TB[:, 0:256], tri, one, start=True, stop=True), signal=False)
            m = pe.run(lambda e: e.matmul(TB[:, 256:512], ones[:, :], one, start=True, stop=True))
            step(lambda e: e.tensor_copy(cnt, TB[:, 256:512]), m)
            t["TB free"] = step(lambda e: e.tensor_copy(pref, TB[:, 0:256]))
            step(lambda e: e.tensor_tensor_scan(cum, cst[:, C_NOTFIRST:C_NOTFIRST + 256], cnt, 0.0,
                                                ALU.mult, ALU.add))
            step(lambda e: e.tensor_tensor(pref, pref, cum, ALU.add))
            step(lambda e: e.tensor_tensor(pref, pref, cnt, ALU.subtract))
            total = cum.rearrange("p (e k) -> p e k", e=E)[:, :, NBLK - 1:NBLK].broadcast_to([P, E, NBLK])
            thr = cst[:, C_THR:C_THR + NBLK].unsqueeze(1).broadcast_to([P, E, NBLK])
            step(lambda e: e.tensor_tensor(tmp.rearrange("p (e k) -> p e k", e=E), total, thr, ALU.is_gt))
            ntile, end, first = small[:, 0:E], small[:, E:2 * E], small[:, 2 * E:3 * E]
            step(lambda e: e.tensor_reduce(ntile, tmp.rearrange("p (e k) -> p e k", e=E), AX_X, ALU.add))
            step(lambda e: e.tensor_tensor_scan(end, ones[:, 0:E], ntile, 0.0, ALU.mult, ALU.add), t["ones"])
            step(lambda e: e.tensor_tensor(first, end, ntile, ALU.subtract))
            step(lambda e: e.scalar_tensor_tensor(
                pref.rearrange("p (e k) -> p e k", e=E), first.unsqueeze(2).broadcast_to([P, E, NBLK]), float(P),
                pref.rearrange("p (e k) -> p e k", e=E), ALU.mult, ALU.add))
            step(lambda e: e.tensor_tensor(pref, pref, one, ALU.mult))
            step(lambda e: e.tensor_reduce(low, pref.rearrange("p (e k) -> p k e", e=E), AX_X, ALU.add))
            t["pos"] = step(lambda e: e.tensor_copy(pos_u[:, :], low))
            te = scratch(6, NTILE * E)
            step(lambda e: e.tensor_tensor(
                te.rearrange("p (n e) -> p n e", e=E), end.unsqueeze(1).broadcast_to([P, NTILE, E]),
                cst[:, C_TILE:C_TILE + NTILE].unsqueeze(2).broadcast_to([P, NTILE, E]), ALU.is_le))
            step(lambda e: e.tensor_reduce(tmp[:, 0:NTILE], te.rearrange("p (n e) -> p n e", e=E), AX_X, ALU.add))
            t["tile expert"] = step(lambda e: e.tensor_scalar(ej_i[:, :], tmp[:, 0:NTILE], float(E - 1), None,
                                                              ALU.min))

        def scatter(c):
            sp.wait(t["xn stored"], t.get(("scattered", c - 2)))
            src = attn_in[:, c % 2, :, :]
            got = dma(src, by_batch(xn_d, c), "regather", c % 2)
            pool.wait(got, t["pos"], t["sorted clear"])
            for k in range(KB):
                if ("scatter", c % 2) not in fl:
                    fl["scatter", c % 2] = flow(f"dma_scatter{c % 2}")
                t["scattered", c] = pool.run(lambda e, k=k: e.indirect_dma_start(
                    out=sorted_d, out_offset=bass.IndirectOffsetOnAxis(
                        ap=pos_u[:, c * KB + k:c * KB + k + 1], axis=0),
                    in_=src[:, k, :], in_offset=None), flow=fl["scatter", c % 2], by=16)

        def expert_load(n):
            w = n % NW
            sp.wait(t["scattered", NB - 2], t["scattered", NB - 1], t["tile expert"], t.get(("down mm", n - NW)),
                    t.get(("turn xs", n - 2)))
            t["xs", n] = dma(xs[:, n % 2, :], sorted_d[n * P:(n + 1) * P, :], "xs", n % 2)

            def load(e, dst, src):
                ex = e.value_load(ej_i[0:1, n:n + 1], min_val=0, max_val=E - 1)
                return e.dma_start(dst, src[bass.ds(ex, 1)].rearrange("a p c -> p (a c)"))

            for dst, src in ((gu_w[:, w, :, :].rearrange("p a c -> p (a c)"), gate_up),
                             (dn_w[:, w, :, :].rearrange("p a c -> p (a c)"), down)):
                key = f"dma_experts{w}"
                if key not in fl:
                    fl[key] = flow(key)
                t["weights", n] = sp.run(lambda e, dst=dst, src=src: load(e, dst, src), flow=fl[key], by=16)

        def expert_turn(n):
            pe.wait(t["xs", n], t["TB free"])
            t["turn xs", n] = pe.run(lambda e: e.transpose(TB[:, 0:P], xs[:, n % 2, :], ident))

        def expert_xT(n):
            act.wait(t["turn xs", n], t.get(("up mm", n - 2)))
            t["xsT", n] = act.run(lambda e: e.copy(xsT[:, n % 2, :], TB[:, 0:P]))
            t["TB free"] = t["xsT", n]

        def expert_up(n):
            w = n % NW
            pe.wait(t["xsT", n], t["weights", n], t.get(("acted", n - 1)))
            for a, dst in ((0, GB), (1, UB)):
                for c in range(NCH):
                    m = pe.run(lambda e, a=a, c=c, dst=dst: e.matmul(
                        dst[:, c * P:(c + 1) * P], gu_w[:, w, a, c * P:(c + 1) * P], xsT[:, n % 2, :],
                        start=True, stop=True), signal=c == NCH - 1)
                if a == 0:
                    t["gate mm", n] = m
            t["up mm", n] = m

        def expert_tanh(n):
            act.wait(t["gate mm", n], t.get(("acted", n - 2)))
            t["th_f", n] = act.run(lambda e: e.activation(th_f[:, n % 2, :], GB[:, 0:IFP], ACT.Tanh, scale=0.5))

        def expert_act(n):
            dve.wait(t["th_f", n], t.get(("down mm", n - 2)), t["sorted clear"])
            m = dve.run(lambda e: e.scalar_tensor_tensor(th_f[:, n % 2, :], th_f[:, n % 2, :], 1.0, GB[:, 0:IFP],
                                                         ALU.add, ALU.mult))
            dve.wait(m, t["up mm", n])
            t["acted", n] = dve.run(lambda e: e.scalar_tensor_tensor(
                act_f[:, n % 2, :], th_f[:, n % 2, :], 0.5, UB[:, 0:IFP], ALU.mult, ALU.mult))

        def expert_down(n):
            w = n % NW
            pe.wait(t["acted", n], t["TB free"])
            for c in range(NCH):
                m = pe.run(lambda e, c=c: e.matmul(TB[:, 0:H], act_f[:, n % 2, c * P:(c + 1) * P], dn_w[:, w, c, :],
                                                   start=(c == 0), stop=(c == NCH - 1)), signal=c == NCH - 1)
            t["down mm", n] = m

        def expert_out(n):
            act.wait(t["down mm", n], t.get(("ys stored", n - 2)))
            t["TB free"] = act.run(lambda e: e.copy(ys[:, n % 2, :], TB[:, 0:H]))
            sp.wait(t["TB free"])
            t["ys stored", n] = dma(ffn_d[n * P:(n + 1) * P, :], ys[:, n % 2, :], "ysout", n % 2)

        def gather(b):
            k2 = b % 2
            pool.wait(t["ys stored", NTILE - 2], t["ys stored", NTILE - 1], t.get(("out stored", b - 2)),
                      t["xt free"], t["xn stored"], t["xn read"])
            if ("gather", k2) not in fl:
                fl["gather", k2] = flow(f"dma_gather{k2}")
            for k in range(KB):
                t["gathered", b] = pool.run(lambda e, k=k: e.indirect_dma_start(
                    out=fin[k2][:, k, :], out_offset=None, in_=ffn_d,
                    in_offset=bass.IndirectOffsetOnAxis(ap=pos_u[:, b * KB + k:b * KB + k + 1], axis=0)),
                    flow=fl["gather", k2], by=16)

        def final_load(b):
            k2 = b % 2
            sp.wait(t["attn stored", b], t.get(("out stored", b - 2)), t["scattered", NB - 2 + k2])
            t["attn in", b] = dma(attn_in[:, k2, :, :], by_batch(attn_d, b), "attnin", k2)

        def final(b):
            k2 = b % 2
            dve.wait(t["attn in", b], t["gathered", b])
            m = dve.run(lambda e: e.tensor_tensor(fin[k2][:, :, :], fin[k2][:, :, :], attn_in[:, k2, :, :], ALU.add))
            sp.wait(m)
            t["out stored", b] = dma(by_batch(out, b), fin[k2][:, :, :], "out", k2)

        later = {}

        def at(step, fn, *a):
            later.setdefault(step, []).append((fn, a))

        def front(v, s0=None):
            plan = [(-8, batch_turn, v // 2)] if v % 2 == 0 else []
            plan += [(-7, in_proj, v, 0, 0), (-6, in_proj, v, 0, 1), (-5, in_proj, v, 1, 0), (-4, in_proj, v, 1, 1),
                     (-4, xi_act, v, 0), (-2, xi_act, v, 1), (-2, xi_mul, v, 0), (0, xi_mul, v, 1),
                     (-2, z_proj, v, 0), (0, z_proj, v, 1), (0, z_act, v, 0), (2, z_act, v, 1),
                     (1, x_proj, v), (2, z_mul, v, 0), (3, z_mul, v, 1), (3, dbc_out, v),
                     (4, dt_proj, v), (5, BC_load, v), (6, softplus, v), (8, delta_out, v),
                     (10, pair_load, v, 0), (12, pair_load, v, 1)]
            for k, fn, *a in sorted(plan, key=lambda x: x[0]):
                if s0 is None:
                    fn(*a, *([dve] if fn is delta_out else []))
                else:
                    at(max(0, s0 + k), fn, *a)

        ln_first(0)
        ln_second(0)
        prepare_front()
        ln_third(0)
        prepare_A()
        front(0)
        prepare_rest()
        clear_sorted()
        for c in range(1, NB):
            s0 = LN_STEPS * (c - 1) - 2
            at(max(0, s0), ln_load, c)
            at(s0 + 3, ln_first, c)
            at(s0 + 5, ln_second, c)
            at(s0 + 7, ln_third, c)
        for u in range(UNITS):
            s0 = NSTEP * u
            at(s0, pair_load, u, 2)
            at(s0 + 4, pair_load, u, 3)
            if u + 1 < UNITS:
                front(u + 1, s0)
                if u % 2 == 0 and u + 2 < UNITS:
                    at(s0 + 6, batch_load, (u + 2) // 2)
            at(s0 + 12, gate, u, 0)
            at(s0 + NSTEP + 3, gate, u, 1)
            if u % 2 == 1:
                at(s0 + NSTEP - 2, base_load, u // 2)
                for k in range(KB):
                    at(s0 + NSTEP + 5 + k, out_mm, u // 2, k)
                at(s0 + NSTEP + 10, out_add, u // 2)
        r0 = LN_STEPS * (NB - 1) + 2
        at(r0, route)
        for c in range(NB):
            at(r0 + 2 + 2 * c, scatter, c)
        f0, gap = r0 + 20, 3
        for n in range(NTILE):
            s0 = f0 + gap * n
            for k, fn in ((0, expert_load), (3, expert_turn), (4, expert_xT), (5, expert_up), (6, expert_tanh),
                          (8, expert_act), (9, expert_down), (9, expert_out)):
                at(s0 + k, fn, n)
        g0 = f0 + gap * NTILE + 10
        last = UNITS * NSTEP
        for b in range(NB):
            s0 = max(g0 + 4 * b, NSTEP * (2 * b + 2) + 12)
            at(s0, gather, b)
            at(s0, final_load, b)
            at(s0 + 5, final, b)
        for m in range(LEAD):
            decay(0, m)
        du_B(0, 0)
        m = 0
        while m < last + SUM_LAG or any(k >= m for k in later):
            if m + LEAD < last:
                decay(*divmod(m + LEAD, NSTEP))
            for fn, a in later.get(m, ()):
                fn(*a)
            if m < last:
                u, s = divmod(m, NSTEP)
                if m + 1 < last:
                    du_B(*divmod(m + 1, NSTEP))
                scan(u, s)
                times_C(u, s)
            if m >= SUM_LAG and (m - SUM_LAG) % 2 and m - SUM_LAG < last:
                u, s = divmod(m - SUM_LAG, NSTEP)
                if s % 8 == 1:
                    skip_mm(u, s // 8)
                sum_states(u, s)
            m += 1
        for name, f in list(fl.items()):
            sp.wait((f, f.value))

        block = ctx.enter_context(nc.Block())

        @block.sync
        def _(e):
            sp.play(e)

        @block.tensor
        def _(e):
            pe.play(e)

        @block.scalar
        def _(e):
            act.play(e)

        @block.vector
        def _(e):
            dve.play(e)

        @block.gpsimd
        def _(e):
            pool.play(e)


def shape_constants():
    import numpy as np
    c = np.zeros((P, C_END), np.float32)
    c[:, C_ID:C_ID + P] = np.eye(P)
    c[:, C_TRI:C_TRI + P] = np.triu(np.ones((P, P)), 1)
    c[:, C_SEL:C_SEL + DD] = np.tile(np.eye(DD), (G, 1))
    c[:, C_IOTA:C_IOTA + E] = np.arange(E)
    c[:, C_THR:C_THR + NBLK] = P * np.arange(NBLK)
    c[:, C_NOTFIRST:C_NOTFIRST + E * NBLK] = np.tile(np.arange(NBLK) > 0, E)
    c[:, C_TILE:C_TILE + NTILE] = np.arange(NTILE)
    return c


def kernel(**inputs):
    import numpy as np
    import concourse.bacc as bacc
    from concourse.bass_utils import run_bass_kernel_spmd

    a = {k: np.asarray(v) for k, v in inputs.items()}

    def both(name, lay):
        return np.ascontiguousarray(np.stack([lay(a[f"L0_attn_{d}_{name}"]) for d in "fb"]))

    def halves(v):
        return v.reshape(2, P).T

    gate_up = np.zeros((E, P, 2, IFP), np.float32)
    gate_up[:, :, 0, :IF] = a["L0_ffn_gate_w"].transpose(0, 2, 1)
    gate_up[:, :, 1, :IF] = a["L0_ffn_up_w"].transpose(0, 2, 1)
    down = np.zeros((E, IFP, H), np.float32)
    down[:, :IF] = a["L0_ffn_down_w"].transpose(0, 2, 1)
    arrays = {
        "x": a["L0_attn_x"].reshape(NBLK * P, H),
        "in_wT": both("in_w", lambda w: w.T).transpose(1, 0, 2),
        "conv_wT": both("conv_w", lambda w: w.T).reshape(2 * NTAP * DI),
        "x_wT": both("x_w", lambda w: w.T.reshape(2, P, NDBC).transpose(1, 0, 2)).transpose(1, 0, 2, 3),
        "dt_wT": both("dt_w", lambda w: w.T).transpose(1, 0, 2),
        "A_log": both("A_log", lambda w: w.reshape(J, DD, G, R).transpose(2, 1, 0, 3).reshape(P, J, R))
        .transpose(1, 0, 2, 3),
        "out_w": both("out_w", lambda w: w).transpose(1, 0, 2),
        "comb_wT": a["L0_attn_combine_w"].T.reshape(2, P, H).transpose(1, 0, 2),
        "comb_b": a["L0_attn_combine_b"].reshape(1, H),
        "col_vectors": np.concatenate(
            [both(n, halves).transpose(1, 0, 2).reshape(P, 4) for n in ("conv_b", "dt_b", "D")]
            + [a["L0_attn_ln_g"].reshape(P, 1), a["L0_attn_ln_b"].reshape(P, 1)], axis=1),
        "router_wT": a["L0_ffn_router_w"].T,
        "gate_up": gate_up.reshape(E, P, 2 * IFP),
        "down": down.reshape(E, NCH, P, H).transpose(0, 2, 1, 3).reshape(E, P, NCH * H),
        "consts": shape_constants(),
    }
    nc = bacc.Bacc("TRN2", target_bir_lowering=False, num_devices=1)
    fed, args = {}, []
    for name, v in arrays.items():
        v = np.ascontiguousarray(v)
        fed["in_" + name] = v
        args.append(nc.dram_tensor("in_" + name, v.shape, mybir.dt.from_np(v.dtype), kind="ExternalInput").ap())
    out = nc.dram_tensor("out_0", (NBLK * P, H), F32, kind="ExternalOutput").ap()
    mamba_moe_kernel(nc, *args, out)
    r = run_bass_kernel_spmd(nc, [fed], core_ids=[0])
    return r.results[0]["out_0"].reshape(NB, L, H)
```

```python
from contextlib import ExitStack

import concourse.bass as bass
from concourse import mybir

F32 = mybir.dt.float32
I32 = mybir.dt.int32
U32 = mybir.dt.uint32
ALU = mybir.AluOpType
ACT = mybir.ActivationFunctionType
AX_X = mybir.AxisListType.X

P = 128
NB, L, H = 8, 512, 128
KB = L // P
NBLK = NB * KB
DI, DS, DR, NTAP = 256, 16, 8, 4
NDBC = DR + 2 * DS
G, DD = 4, 32
R = DS // G
J = DI // DD
RH = 2
NSTEP = J * R // RH
UNITS = 2 * NB
E, IF, IFP = 8, 352, 384
NCH = IFP // P
NTILE = NBLK + E - 1
EPS = 1e-5

C_ID, C_TRI, C_SEL, C_IOTA, C_THR, C_NOTFIRST, C_TILE = 0, 128, 256, 288, 296, 328, 584
C_END = C_TILE + NTILE
NCOL = 14


class Flow:

    def __init__(self, sem):
        self.sem, self.value = sem, 0


class Queue:

    def __init__(self, own):
        self.ops, self.own, self.met = [], own, {}

    def wait(self, *marks):
        for mark in marks:
            if mark is None:
                continue
            flow, value = mark
            if self.met.get(id(flow), 0) >= value:
                continue
            self.met[id(flow)] = value
            self.ops.append(lambda e, s=flow.sem, v=value: e.wait_ge(s, v))

    def run(self, fn, signal=True, flow=None, by=1):
        if not signal:
            self.ops.append(fn)
            return None
        flow = flow or self.own
        flow.value += by
        self.ops.append(lambda e: fn(e).then_inc(flow.sem, by))
        return flow, flow.value

    def play(self, e):
        for op in self.ops:
            op(e)


def mamba_moe_kernel(nc, x, in_wT, conv_wT, x_wT, dt_wT, A_log, out_w, comb_wT, comb_b,
                     col_vectors, router_wT, gate_up, down, consts, out):
    ctx = ExitStack()
    with ctx:
        def sb(name, shape, dt=F32):
            return ctx.enter_context(nc.sbuf_tensor(name, shape, dt))

        def flow(name):
            return Flow(ctx.enter_context(nc.semaphore(name)))

        def dram(name, shape, dt=F32):
            return nc.dram_tensor(name, shape, dt, kind="Internal").ap()

        xn_d = dram("xn_scratch", (NBLK * P, H))
        xn2_d = dram("xn2_scratch", (NBLK * P, H))
        base_d = dram("base_scratch", (NBLK * P, H))
        attn_d = dram("attn_scratch", (NBLK * P, H))
        sorted_d = dram("sorted_tokens", (NTILE * P, H))
        ffn_d = dram("sorted_ffn", (NTILE * P, H))
        delta_d = dram("delta_scratch", (2, DD, J, L))
        du_d = dram("du_scratch", (2, DD, J, L))
        dbc_d = dram("dbc_scratch", (2, NDBC, L))

        def by_batch(t, b):
            return t.rearrange("(b k p) h -> b p k h", b=NB, p=P)[b]

        cst = sb("cst", [P, C_END])
        ones = sb("ones", [P, P])
        neg_half = sb("neg_half", [P, KB])
        w_in = sb("w_in", [P, 2, NTAP + 1, DI])
        w_x = sb("w_x", [P, 2, 2, NDBC])
        w_dt = sb("w_dt", [DR, 2, DI])
        diag_D = sb("diag_D", [P, 2, 2, P])
        w_out = sb("w_out", [P, 2, 2, H])
        cols = sb("cols", [P, 16])
        A_sb = sb("A_sb", [P, 2, J, R])
        rw = sb("rw", [P, E])
        comb_bias = sb("comb_bias", [1, H])
        xn = sb("xn", [P, KB, H])
        xn2 = sb("xn2", [P, KB, H])
        stats = sb("stats", [P, KB, 6])
        moments = sb("moments", [P, KB, 2])
        moments2 = sb("moments2", [P, KB, 2])
        rstd = sb("rstd", [P, KB])
        rstd2 = sb("rstd2", [P, KB])
        xnT = sb("xnT", [P, L])
        xn2_in = sb("xn2_in", [P, KB, H])
        xpad = sb("xpad", [P, 2, L + 6])
        xi = sb("xi", [P, 2, 2, L])
        tmpA = sb("tmpA", [P, 2, L])
        tmpB = sb("tmpB", [P, 2, L])
        du = tmpB
        zs = sb("zs", [P, 2, 2, L])
        dbc = sb("dbc", [NDBC, L])
        NP = 3
        delta_rep = sb("delta_rep", [P, NP, 2, L])
        du_rep = sb("du_rep", [P, NP, 2, L])
        B_rep = sb("B_rep", [P, 2, R, L])
        C_rep = sb("C_rep", [P, 2, R, L])
        NA, NH = 4, 8
        LEAD = 3
        SUM_LAG = 2
        LATE = 2
        LN_ONE, LN_MORE, LN_START, LN_GAP = (0, 1, 3, 5), (0, 4, 9, 12), 1, 6
        dA = sb("dA", [P, NA, RH * L + 1])
        hs = sb("hs", [P, NH, RH * L])
        yg = sb("yg", [P, 2, 2, L])
        base_in = sb("base_in", [P, KB, H])
        NW = 3
        gu_w = sb("gu_w", [P, NW, 2, IFP])
        dn_w = sb("dn_w", [P, NW, NCH, H])
        xs = sb("xs", [P, 2, H])
        xsT = sb("xsT", [P, 2, P])
        th_f = sb("th_f", [P, 2, IFP])
        act_f = sb("act_f", [P, 2, IFP])
        ys = sb("ys", [P, 2, H])
        fin = (sb("fin", [P, KB, H]), xn)
        attn_in = sb("attn_in", [P, 2, KB, H])
        xin = attn_in
        logits = sb("logits", [P, NBLK, E])
        pos_u = sb("pos_u", [P, NBLK], U32)
        ej_i = sb("ej_i", [P, NTILE], I32)
        small = sb("small", [P, 64])

        def bank(name):
            return ctx.enter_context(nc.psum_tensor(name, [P, 512], F32))

        Y = [bank("y0"), bank("y1")]
        FB = [bank("front0"), bank("front1")]
        MB = bank("mixed")
        GB, UB, TB = bank("gate"), bank("up"), bank("turn")

        pe, act, dve, pool, sp = (Queue(flow("done_" + n)) for n in ("pe", "act", "dve", "pool", "sp"))
        fl = {}

        def dma(dst, src, name, k=0, q=None):
            key = f"dma_{name}{k}"
            if key not in fl:
                fl[key] = flow(key)
            return (q or sp).run(lambda e: e.dma_start(dst, src), flow=fl[key], by=16)

        t = {}

        ident = cst[:, C_ID:C_ID + P]
        tri = cst[:, C_TRI:C_TRI + P]
        sel = cst[:, C_SEL:C_SEL + DD]

        cwb = delta_rep[:, :, :, :].rearrange("p a b c -> p (a b c)")[:, 0:2 * NTAP * DI].rearrange(
            "p (d k c) -> p d k c", d=2, k=NTAP)
        inw_t = du_rep[:, :, :, :].rearrange("p a b c -> p (a b c)")[:, 0:2 * 2 * DI].rearrange(
            "p (d c) -> p d c", d=2)
        outw_t = hs[:, 0, 0:2 * DI].rearrange("p (d c) -> p d c", d=2)
        combw_t = hs[:, 1, 0:2 * H].rearrange("p (d o) -> p d o", d=2)
        t["xin", 0] = dma(xin[:, 0, :, :], by_batch(x, 0), "xin", 0)
        dma(cwb.rearrange("p d k c -> p (d k c)"), conv_wT.unsqueeze(0).broadcast_to([P, 2 * NTAP * DI]), "wfront")
        dma(inw_t, in_wT, "wfront")
        dma(cols[:, 0:NCOL], col_vectors, "wfront")
        t["cst"] = front_weights_in = dma(cst[:, :], consts, "wfront")
        dma(w_x[:, :, :, :], x_wT, "w", q=act)
        dma(w_dt[:, :, :], dt_wT, "w", q=act)
        dma(A_sb[:, :, :, :], A_log, "w", q=act)
        dma(outw_t, out_w, "w", q=act)
        dma(combw_t, comb_wT, "w", q=act)
        dma(rw[:, :], router_wT, "w", q=act)
        weights_in = dma(comb_bias[:, :], comb_b, "w", q=act)

        def conv_bias(d, h):
            return cols[:, 2 * d + h:2 * d + h + 1]

        def dt_bias(d, h):
            return cols[:, 4 + 2 * d + h:5 + 2 * d + h]

        t["ones"] = dve.run(lambda e: e.memset(ones[:, :], 1.0))
        t["pow"] = dve.run(lambda e: e.memset(neg_half[:, :], -0.5))
        dve.run(lambda e: e.memset(xpad[:, :, 0:NTAP - 1], 0.0), signal=False)
        t["xpad0"] = dve.run(lambda e: e.memset(xpad[:, :, L + NTAP - 1:], 0.0))
        t["dA0"] = dve.run(lambda e: e.memset(dA[:, :, 0:RH * L + 1:L], 0.0))
        t["sorted0"] = pool.run(lambda e: e.memset(act_f[:, :, :], 0.0))

        def prepare_front():
            dve.wait(front_weights_in)
            for d in range(2):
                t["w_in"] = dve.run(lambda e, d=d: e.scalar_tensor_tensor(
                    w_in[:, d, 0:NTAP, :], inw_t[:, d, 0:DI].unsqueeze(1).broadcast_to([P, NTAP, DI]), 0.5,
                    cwb[:, d, :, :], ALU.mult, ALU.mult))
                t["w_in"] = dve.run(lambda e, d=d: e.tensor_scalar(
                    w_in[:, d, NTAP, :], inw_t[:, d, DI:2 * DI], 0.5, None, ALU.mult))
            t["conv_bias"] = dve.run(lambda e: e.tensor_scalar(cols[:, 0:4], cols[:, 0:4], 0.5, None, ALU.mult))

        def prepare_A():
            act.wait(weights_in)
            m = act.run(lambda e: e.activation(A_sb[:, :, :, :], A_sb[:, :, :, :], ACT.Exp))
            act.wait(m)
            t["A"] = act.run(lambda e: e.mul(A_sb[:, :, :, :], A_sb[:, :, :, :], -1.0))

        def prepare_rest():
            dve.wait(front_weights_in)
            for d in range(2):
                for h in range(2):
                    t["diag"] = dve.run(lambda e, d=d, h=h: e.tensor_scalar(
                        diag_D[:, d, h, :], ident, cols[:, 8 + 2 * d + h:9 + 2 * d + h], None, ALU.mult))
            pe.wait(weights_in)
            for d in range(2):
                for h in range(2):
                    m = pe.run(lambda e, d=d, h=h: e.matmul(
                        MB[:, (2 * d + h) * H:(2 * d + h + 1) * H], outw_t[:, d, h * P:(h + 1) * P],
                        combw_t[:, d, :], start=True, stop=True))
            dve.wait(m)
            t["w_out"] = dve.run(lambda e: e.tensor_copy(
                w_out[:, :, :, :].rearrange("p d h o -> p (d h o)"), MB[:, :]))
            t["MB free"] = t["staging"] = t["w_out"]

        def moments_of(src, mark, mom, r, used):
            dve.wait(mark, used)
            for k in range(KB):
                s = dve.run(lambda e, k=k: e.bn_stats(stats[:, k, :], src[:, k, :]))
            dve.wait(s)
            for k in range(KB):
                m = dve.run(lambda e, k=k: e.bn_aggr(mom[:, k, :], stats[:, k, :]))
            dve.wait(m)
            v = dve.run(lambda e: e.tensor_scalar(r[:, :], mom[:, :, 1], EPS, None, ALU.add))
            pool.wait(v, t["pow"])
            return pool.run(lambda e: e.tensor_tensor(r[:, :], r[:, :], neg_half[:, :], ALU.pow))

        def normalize(dst, src, mom, r):
            for k in range(KB):
                m = dve.run(lambda e, k=k: e.tensor_scalar(
                    dst[:, k, :], src[:, k, :], mom[:, k, 0:1], r[:, k:k + 1], ALU.subtract, ALU.mult))
            return m

        def ln_load(c):
            sp.wait(t.get(("base stored", c - 2)))
            t["xin", c] = dma(xin[:, c % 2, :, :], by_batch(x, c), "xin", c % 2)

        def ln_first(c):
            t["rstd"] = moments_of(xin[:, c % 2, :, :], t["xin", c], moments, rstd, t.get("xn"))

        def ln_second(c):
            dve.wait(t["rstd"], t.get("xn stored"), t.get("xn2"), t.get("xn turned"))
            t["xn"] = normalize(xn, xin[:, c % 2, :, :], moments, rstd)
            t["rstd2"] = moments_of(xn, t["xn"], moments2, rstd2, t.get("xn2"))
            pool.wait(t["xn"])
            t["base"] = pool.run(lambda e: e.tensor_tensor(
                xin[:, c % 2, :, :], xin[:, c % 2, :, :], xn[:, :, :], ALU.add))
            sp.wait(t["xn"])
            t["xn stored"] = dma(by_batch(xn_d, c), xn[:, :, :], "xnout")
            sp.wait(t["base"])
            t["base stored", c] = dma(by_batch(base_d, c), xin[:, c % 2, :, :], "baseout", c % 2)
            pe.wait(t["xn"], t["cst"], t.get("TB free"))
            for k in range(KB):
                m = pe.run(lambda e, k=k: e.transpose(TB[:, k * P:(k + 1) * P], xn[:, k, :], ident))
            t["xn turned"] = m
            act.wait(m, t.get("logits mm"))
            t["xnT"] = act.run(lambda e: e.copy(xnT[:, :], TB[:, :]))

        def ln_third(c):
            dve.wait(t["rstd2"], t.get("xn2 stored"), t.get("xn2 turned"))
            m = normalize(xn2, xn, moments2, rstd2)
            sp.wait(m)
            t["xn2 stored"] = dma(by_batch(xn2_d, c), xn2[:, :, :], "xn2out")
            t["xn2 in dram", c] = t["xn2 stored"]
            t["xn2"] = m
            pe.wait(t["xnT"], weights_in)
            for k in range(KB):
                m = pe.run(lambda e, k=k: e.matmul(TB[:, k * E:(k + 1) * E], xnT[:, k * P:(k + 1) * P], rw[:, :],
                                                   start=True, stop=True))
            t["logits mm"] = m
            act.wait(m)
            t["TB free"] = act.run(lambda e: e.copy(
                logits[:, c * KB:(c + 1) * KB, :].rearrange("p k e -> p (k e)"), TB[:, 0:KB * E]))
            t["logits"] = t["TB free"]

        def batch_load(b):
            sp.wait(t["xn2 in dram", b], t.get("xn2_in free"))
            t["xn2_in"] = dma(xn2_in[:, :, :], by_batch(xn2_d, b), "xn2in")

        def batch_turn(b):
            src = xn2_in if b else xn2
            pe.wait(t["xn2_in"] if b else t["xn2"], t["cst"], t.get(("FB free", 0)))
            for k in range(KB):
                m = pe.run(lambda e, k=k: e.transpose(FB[0][:, k * P:(k + 1) * P], src[:, k, :], ident))
            t["xn2_in free" if b else "xn2 turned"] = m
            act.wait(m, t["xpad0"], front_weights_in, t.get(("in proj", 2 * b - 3)))
            t["xpad", b] = act.run(lambda e: e.activation(
                xpad[:, b % 2, 3:3 + L], FB[0][:, :], ACT.Identity, scale=cols[:, 12:13], bias=cols[:, 13:14]))
            t["FB free", 0] = t["xpad", b]

        def in_proj(v, h, part=None):
            b, d = divmod(v, 2)
            pe.wait(t["xpad", b], t["w_in"], t.get(("FB free", 1 - h)))
            for k in range(NTAP) if part is None else range(2 * part, 2 * part + 2):
                at = k if d == 0 else 2 * (NTAP - 1) - k
                m = pe.run(lambda e, k=k, at=at: e.matmul(
                    FB[1 - h][:, :], w_in[:, d, k, h * P:(h + 1) * P], xpad[:, b % 2, at:at + L],
                    start=(k == 0), stop=(k == NTAP - 1)), signal=k == NTAP - 1)
            t["in", v, h] = m

        def z_proj(v, h):
            b, d = divmod(v, 2)
            pe.wait(t["FB free", 1 - h])
            t["z", v, h] = pe.run(lambda e: e.matmul(
                FB[1 - h][:, :], w_in[:, d, NTAP, h * P:(h + 1) * P], xpad[:, b % 2, 3:3 + L],
                start=True, stop=True))
            t["in proj", v] = t["z", v, h]

        def xi_act(v, h):
            act.wait(t["in", v, h], t["conv_bias"], t.get(("du stored", v - 1, h)))
            act.run(lambda e: e.activation(tmpA[:, h, :], FB[1 - h][:, :], ACT.Identity,
                                           bias=conv_bias(v % 2, h)), signal=False)
            t["th", v, h] = act.run(lambda e: e.activation(tmpB[:, h, :], FB[1 - h][:, :], ACT.Tanh,
                                                           bias=conv_bias(v % 2, h)))
            t["FB free", 1 - h] = t["th", v, h]

        def xi_mul(v, h):
            dve.wait(t["th", v, h], t.get(("D mm", v - 2)), t.get(("du made", v - 2)))
            t["xi", v, h] = dve.run(lambda e: e.scalar_tensor_tensor(
                xi[:, v % 2, h, :], tmpB[:, h, :], 1.0, tmpA[:, h, :], ALU.add, ALU.mult))

        def z_act(v, h):
            act.wait(t["z", v, h], t["xi", v, h])
            t["thz", v, h] = act.run(lambda e: e.activation(tmpB[:, h, :], FB[1 - h][:, :], ACT.Tanh))

        def z_mul(v, h):
            dve.wait(t["thz", v, h], t.get(("gated", 2 * (v - 2) + h)))
            t["zs", v, h] = dve.run(lambda e: e.scalar_tensor_tensor(
                zs[:, v % 2, h, :], tmpB[:, h, :], 1.0, FB[1 - h][:, :], ALU.add, ALU.mult))
            t["FB free", 1 - h] = t["zs", v, h]

        def x_proj(v):
            d = v % 2
            pe.wait(t["xi", v, 0], t["xi", v, 1], weights_in, t["MB free"])
            for h in range(2):
                m = pe.run(lambda e, h=h: e.matmul(MB[0:NDBC, :], w_x[:, d, h, :], xi[:, v % 2, h, :],
                                                   start=(h == 0), stop=(h == 1)), signal=h == 1)
            t["dbc mm"] = m

        def dbc_out(v):
            act.wait(t["dbc mm"], t.get("dbc stored"), t.get(("dt", v - 1, 1)))
            t["dbc"] = act.run(lambda e: e.copy(dbc[:, :], MB[0:NDBC, :]))
            t["MB free"] = t["dbc"]
            sp.wait(t["dbc"], t.get(("BC", v - 2)))
            t["dbc stored"] = dma(dbc_d[v % 2], dbc[:, :], "dbcout")

        def dt_proj(v):
            d = v % 2
            pe.wait(t["dbc"])
            for h in range(2):
                pe.wait(t["FB free", 1 - h])
                t["dt", v, h] = pe.run(lambda e, h=h: e.matmul(
                    FB[1 - h][:, :], w_dt[:, d, h * P:(h + 1) * P], dbc[0:DR, :], start=True, stop=True))

        def softplus(v):
            for h in range(2):
                act.wait(t["dt", v, h], t["xi", v, h], t["zs", v, h])
                act.run(lambda e, h=h: e.activation(tmpA[:, h, :], FB[1 - h][:, :], ACT.Relu,
                                                    bias=dt_bias(v % 2, h)), signal=False)
                m = t["FB free", 1 - h] = act.run(lambda e, h=h: e.activation(
                    tmpB[:, h, :], FB[1 - h][:, :], ACT.Abs, bias=dt_bias(v % 2, h)))
            act.wait(m)
            m = act.run(lambda e: e.activation(tmpB[:, :, :], tmpB[:, :, :], ACT.Exp, scale=-1.0))
            act.wait(m)
            for h in range(2):
                t["log", v, h] = act.run(lambda e, h=h: e.activation(tmpB[:, h, :], tmpB[:, h, :], ACT.Ln, bias=1.0))

        def BC_load(v):
            k = v % 2
            sp.wait(t["dbc stored"], t.get(("mult", v - 2, NSTEP - 1)), t.get(("C mult", v - 2, NSTEP - 1)))
            for dst, row in ((B_rep, DR), (C_rep, DR + DS)):
                t["BC", v] = dma(dst[:, k, :, :].rearrange("p r t -> p (r t)"),
                                 dbc_d[k, row:row + DS, :].rearrange("(g r) t -> g (r t)", g=G)
                                 .unsqueeze(1).broadcast_to([G, DD, R * L]), "bc", k)

        def delta_out(v, eng=None):
            eng, k = eng or pool, v % 2
            for h in range(2):
                eng.wait(t["log", v, h])
                t["delta", v, h] = eng.run(lambda e, h=h: e.tensor_tensor(
                    tmpA[:, h, :], tmpA[:, h, :], tmpB[:, h, :], ALU.add))
                eng.wait(t["delta", v, h], t["xi", v, h])
                t["du made", v] = t["du made", v, h] = eng.run(lambda e, h=h: e.tensor_tensor(
                    du[:, h, :], tmpA[:, h, :], xi[:, k, h, :], ALU.mult))
                sp.wait(t["delta", v, h], t.get(("pair", 4 * (v - 2) + 3)))
                dma(delta_d[k].rearrange("e j t -> j e t")[4 * h:4 * h + 4], tmpA[:, h, :], "dout", h)
                sp.wait(t["du made", v])
                t["du stored", v, h] = dma(
                    du_d[k].rearrange("e j t -> j e t")[4 * h:4 * h + 4], du[:, h, :], "dout", h)

        def pair_load(v, p):
            k, q = v % 2, 4 * v + p
            sp.wait(t["du stored", v, p // 2], t.get(("pair used", q - NP)), t["w_in"])
            for dst, src in ((delta_rep, delta_d), (du_rep, du_d)):
                t["pair", q] = dma(dst[:, q % NP, :, :].rearrange("p j t -> p (j t)"),
                                   src[k, :, 2 * p:2 * p + 2, :].rearrange("e j t -> e (j t)")
                                   .unsqueeze(0).broadcast_to([G, DD, 2 * L]), "pair", q % NP)

        def first_pair():
            for src, made, banks, eng, free in (
                    (tmpA, t["delta", 0, 0], (GB, UB), act, t["w_in"]),
                    (du, t["du made", 0, 0], (TB, MB), dve, t["MB free"])):
                pe.wait(made, t["cst"], t["TB free"], free)
                for j in range(2):
                    for g in range(G):
                        m = pe.run(lambda e, j=j, g=g, src=src, bank=banks[j]: e.matmul(
                            bank[g * DD:(g + 1) * DD, :], ident[:, j * DD:(j + 1) * DD], src[:, 0, :],
                            start=True, stop=True, skip_group_check=True), signal=g == G - 1)
                    eng.wait(m, t["w_in"])
                    if eng is act:
                        t["pair", 0] = act.run(lambda e, j=j: e.copy(delta_rep[:, 0, j, :], (GB, UB)[j][:, :]))
                    else:
                        t["first du"] = dve.run(lambda e, j=j: e.tensor_copy(
                            du_rep[:, 0, j, :], (TB, MB)[j][:, :]))
            t["TB free"] = t["MB free"] = t["first du"]

        def place(s):
            return s // 4, (s // 2) % 2, s % 2

        def decay(u, s):
            p, rh, jj = place(s)
            m, q, d = NSTEP * u + s, 4 * u + p, u % 2
            act.wait(t["pair", q], t["A"], t["dA0"], t.get(("scan", m - NA)))
            src = delta_rep[:, q % NP, jj, 1:L] if d == 0 else delta_rep[:, q % NP, jj, 0:L - 1]
            for r in range(RH):
                i = act.run(lambda e, r=r: e.activation(
                    dA[:, m % NA, r * L + 1:(r + 1) * L], src, ACT.Exp,
                    scale=A_sb[:, d, 2 * p + jj, RH * rh + r:RH * rh + r + 1]), signal=r == RH - 1)
            t["decay", m] = i

        def du_B(u, s):
            p, rh, jj = place(s)
            m, q = NSTEP * u + s, 4 * u + p
            dve.wait(t["pair", q], t["first du"], t["BC", u], t.get(("y mm", m + 1 - NH)), t["staging"])
            t["mult", m] = dve.run(lambda e: e.tensor_tensor(
                hs[:, m % NH:m % NH + 2, :].rearrange("p j (r t) -> p j r t", r=RH),
                du_rep[:, q % NP, :, :].unsqueeze(2).broadcast_to([P, 2, RH, L]),
                B_rep[:, u % 2, RH * rh:RH * rh + RH, :].unsqueeze(1).broadcast_to([P, 2, RH, L]), ALU.mult))
            t["mult", m + 1] = t["mult", u, s] = t["mult", u, s + 1] = t["mult", m]
            t["du read", q] = t["mult", m]

        def scan(u, s):
            m, d, n = NSTEP * u + s, u % 2, RH * L
            dve.wait(t["mult", m], t["decay", m])
            a = dA[:, m % NA, 0:n] if d == 0 else dA[:, m % NA, 1:n + 1][:, ::-1]
            b = hs[:, m % NH, :] if d == 0 else hs[:, m % NH, :][:, ::-1]
            t["scan", m] = dve.run(lambda e: e.tensor_tensor_scan(b, a, b, 0.0, ALU.mult, ALU.add))
            t["pair used", 4 * u + s // 4] = t["scan", m]

        dve_C = range(UNITS * NSTEP - 5, UNITS * NSTEP, 2)

        def times_C(u, s):
            p, rh, jj = place(s)
            m = NSTEP * u + s
            eng = dve if m in dve_C else pool
            eng.wait(t["scan", m], t["BC", u])
            t["C mult", m] = t["C mult", u, s] = eng.run(lambda e: e.tensor_tensor(
                hs[:, m % NH, :], hs[:, m % NH, :],
                C_rep[:, u % 2, RH * rh:RH * rh + RH, :].rearrange("p r t -> p (r t)"), ALU.mult))

        def skip_mm(u, h):
            i = 2 * u + h
            pe.wait(t["xi", u, h], t["diag"], t.get(("gated", i - 2)))
            t["D mm", u] = pe.run(lambda e: e.matmul(Y[i % 2][:, :], diag_D[:, u % 2, h, :], xi[:, u % 2, h, :],
                                                     start=True, stop=False, skip_group_check=True))

        def sum_states(u, s):
            p, rh, jj = place(s)
            m, h = NSTEP * u + s, (2 * p) // 4
            pe.wait(t["C mult", m - 1], t["C mult", m])
            for r in range(RH):
                for w in range(2):
                    c = (2 * p + w) % 4
                    i = pe.run(lambda e, r=r, w=w, c=c: e.matmul(
                        Y[h][c * DD:(c + 1) * DD, :], sel, hs[:, (m - 1 + w) % NH, r * L:(r + 1) * L],
                        start=False, stop=(rh == 1 and r == RH - 1), skip_group_check=True),
                        signal=(r == RH - 1 and w == 1))
            t["y mm", m] = t["y mm", m - 1] = i

        def gate(u, h):
            m = NSTEP * u + 8 * h + 7
            dve.wait(t["y mm", m], t["zs", u, h], t.get(("out mm", u // 2 - 1)))
            t["gated", 2 * u + h] = dve.run(lambda e: e.tensor_tensor(
                yg[:, u % 2, h, :], Y[h][:, :], zs[:, u % 2, h, :], ALU.mult))

        def base_load(b):
            sp.wait(t["base stored", b], t.get("attn stored"))
            t["base in"] = dma(base_in[:, :, :], by_batch(base_d, b), "basein")

        def out_mm(b, i):
            pe.wait(t["gated", 4 * b + i], t["w_out"])
            for k in range(KB):
                m = pe.run(lambda e, k=k: e.matmul(
                    MB[:, k * H:(k + 1) * H], yg[:, i // 2, i % 2, k * P:(k + 1) * P],
                    w_out[:, i // 2, i % 2, :], start=False, stop=(i == 3), skip_group_check=True),
                    signal=k == KB - 1)
            t["out mm", b] = m

        def bias_mm(b):
            pe.wait(weights_in, t["ones"], t["MB free"])
            pe.run(lambda e: e.matmul(MB[:, :].rearrange("p (k h) -> p k h", k=KB), ones[0:1, :],
                                      comb_bias[:, :].unsqueeze(1).broadcast_to([1, KB, H]),
                                      start=True, stop=False, skip_group_check=True), signal=False)

        def out_add(b):
            late = b >= NB - LATE
            dve.wait(t["out mm", b], t["late in", b] if late else t["base in"])
            m = dve.run(lambda e: e.tensor_tensor(base_in[:, :, :].rearrange("p k h -> p (k h)"), MB[:, :],
                                                  base_in[:, :, :].rearrange("p k h -> p (k h)"), ALU.add))
            t["MB free"] = m
            sp.wait(m)
            if late:
                t["attn stored"] = dma(by_batch(out, b), base_in[:, :, :], "attnout")
            else:
                t["attn stored"] = t["attn stored", b] = dma(by_batch(attn_d, b), base_in[:, :, :], "attnout")

        def scratch(i, n=NBLK * E):
            return gu_w[:, i // 3, :, :].rearrange("p a b -> p (a b)")[:, (i % 3) * 256:(i % 3) * 256 + n]

        def clear_sorted():
            sp.wait(t["sorted0"])
            flat = sorted_d.rearrange("(n p) h -> p n h", p=P)
            for n in range(0, NTILE, KB):
                w = min(KB, NTILE - n)
                t["sorted clear"] = dma(flat[:, n:n + w, :],
                                         act_f[:, :, :].rearrange("p a c -> p (a c)")[:, 0:w * H].rearrange(
                                             "p (n h) -> p n h", h=H), "clear")

        def route():
            one, val, pref, cnt, cum, tmp = (scratch(i) for i in range(6))
            ke = "p (k e) -> p k e"
            iota = cst[:, C_IOTA:C_IOTA + E].unsqueeze(1).broadcast_to([P, NBLK, E])
            best, low = small[:, 0:32], small[:, 32:64]

            def step(fn, *marks):
                dve.wait(*marks)
                m = dve.run(fn)
                dve.wait(m)
                return m

            step(lambda e: e.tensor_reduce(best, logits[:, :, :], AX_X, ALU.max), t["logits"], t["cst"])
            step(lambda e: e.tensor_tensor(val.rearrange(ke, e=E), logits[:, :, :],
                                           best.unsqueeze(2).broadcast_to([P, NBLK, E]), ALU.is_ge))
            step(lambda e: e.scalar_tensor_tensor(val.rearrange(ke, e=E), val.rearrange(ke, e=E), -float(E), iota,
                                                  ALU.mult, ALU.add))
            step(lambda e: e.tensor_reduce(low, val.rearrange(ke, e=E), AX_X, ALU.min))
            m = step(lambda e: e.tensor_tensor(one.rearrange("p (e k) -> p k e", e=E), val.rearrange(ke, e=E),
                                               low.unsqueeze(2).broadcast_to([P, NBLK, E]), ALU.is_equal))
            pe.wait(m, t["ones"], t["TB free"])
            pe.run(lambda e: e.matmul(TB[:, 0:256], tri, one, start=True, stop=True), signal=False)
            m = pe.run(lambda e: e.matmul(TB[:, 256:512], ones[:, :], one, start=True, stop=True))
            step(lambda e: e.tensor_copy(cnt, TB[:, 256:512]), m)
            t["TB free"] = step(lambda e: e.tensor_copy(pref, TB[:, 0:256]))
            step(lambda e: e.tensor_tensor_scan(cum, cst[:, C_NOTFIRST:C_NOTFIRST + 256], cnt, 0.0,
                                                ALU.mult, ALU.add))
            step(lambda e: e.tensor_tensor(pref, pref, cum, ALU.add))
            step(lambda e: e.tensor_tensor(pref, pref, cnt, ALU.subtract))
            total = cum.rearrange("p (e k) -> p e k", e=E)[:, :, NBLK - 1:NBLK].broadcast_to([P, E, NBLK])
            thr = cst[:, C_THR:C_THR + NBLK].unsqueeze(1).broadcast_to([P, E, NBLK])
            step(lambda e: e.tensor_tensor(tmp.rearrange("p (e k) -> p e k", e=E), total, thr, ALU.is_gt))
            ntile, end, first = small[:, 0:E], small[:, E:2 * E], small[:, 2 * E:3 * E]
            step(lambda e: e.tensor_reduce(ntile, tmp.rearrange("p (e k) -> p e k", e=E), AX_X, ALU.add))
            step(lambda e: e.tensor_tensor_scan(end, ones[:, 0:E], ntile, 0.0, ALU.mult, ALU.add), t["ones"])
            step(lambda e: e.tensor_tensor(first, end, ntile, ALU.subtract))
            step(lambda e: e.scalar_tensor_tensor(
                pref.rearrange("p (e k) -> p e k", e=E), first.unsqueeze(2).broadcast_to([P, E, NBLK]), float(P),
                pref.rearrange("p (e k) -> p e k", e=E), ALU.mult, ALU.add))
            step(lambda e: e.tensor_tensor(pref, pref, one, ALU.mult))
            step(lambda e: e.tensor_reduce(low, pref.rearrange("p (e k) -> p k e", e=E), AX_X, ALU.add))
            t["pos"] = step(lambda e: e.tensor_copy(pos_u[:, :], low))
            te = scratch(6, NTILE * E)
            step(lambda e: e.tensor_tensor(
                te.rearrange("p (n e) -> p n e", e=E), end.unsqueeze(1).broadcast_to([P, NTILE, E]),
                cst[:, C_TILE:C_TILE + NTILE].unsqueeze(2).broadcast_to([P, NTILE, E]), ALU.is_le))
            step(lambda e: e.tensor_reduce(tmp[:, 0:NTILE], te.rearrange("p (n e) -> p n e", e=E), AX_X, ALU.add))
            t["tile expert"] = step(lambda e: e.tensor_scalar(ej_i[:, :], tmp[:, 0:NTILE], float(E - 1), None,
                                                              ALU.min))

        def scatter_load(c):
            sp.wait(t["xn stored"], t.get(("scattered", c - 2)), t["base stored", NB - 2 + c % 2])
            t["scatter in", c] = dma(attn_in[:, c % 2, :, :], by_batch(xn_d, c), "regather", c % 2)

        def scatter(c, k):
            pool.wait(t["scatter in", c], t["pos"], t["sorted clear"])
            if ("scatter", c % 2) not in fl:
                fl["scatter", c % 2] = flow(f"dma_scatter{c % 2}")
            t["scattered", c] = pool.run(lambda e: e.indirect_dma_start(
                out=sorted_d, out_offset=bass.IndirectOffsetOnAxis(
                    ap=pos_u[:, c * KB + k:c * KB + k + 1], axis=0),
                in_=attn_in[:, c % 2, k, :], in_offset=None), flow=fl["scatter", c % 2], by=16)

        def expert_load(n):
            w = n % NW
            sp.wait(t["scattered", NB - 2], t["scattered", NB - 1], t["tile expert"], t.get(("down mm", n - NW)),
                    t.get(("turn xs", n - 2)))
            t["xs", n] = dma(xs[:, n % 2, :], sorted_d[n * P:(n + 1) * P, :], "xs", n % 2)

            def load(e, dst, src):
                ex = e.value_load(ej_i[0:1, n:n + 1], min_val=0, max_val=E - 1)
                return e.dma_start(dst, src[bass.ds(ex, 1)].rearrange("a p c -> p (a c)"))

            for dst, src in ((gu_w[:, w, :, :].rearrange("p a c -> p (a c)"), gate_up),
                             (dn_w[:, w, :, :].rearrange("p a c -> p (a c)"), down)):
                key = f"dma_experts{w}"
                if key not in fl:
                    fl[key] = flow(key)
                t["weights", n] = sp.run(lambda e, dst=dst, src=src: load(e, dst, src), flow=fl[key], by=16)

        def expert_turn(n):
            pe.wait(t["xs", n], t["TB free"])
            t["turn xs", n] = pe.run(lambda e: e.transpose(TB[:, 0:P], xs[:, n % 2, :], ident))

        def expert_xT(n):
            act.wait(t["turn xs", n], t.get(("up mm", n - 2)))
            t["xsT", n] = act.run(lambda e: e.copy(xsT[:, n % 2, :], TB[:, 0:P]))
            t["TB free"] = t["xsT", n]

        def expert_up(n):
            w = n % NW
            pe.wait(t["xsT", n], t["weights", n], t.get(("acted", n - 1)))
            for a, dst in ((0, GB), (1, UB)):
                for c in range(NCH):
                    m = pe.run(lambda e, a=a, c=c, dst=dst: e.matmul(
                        dst[:, c * P:(c + 1) * P], gu_w[:, w, a, c * P:(c + 1) * P], xsT[:, n % 2, :],
                        start=True, stop=True), signal=c == NCH - 1)
                if a == 0:
                    t["gate mm", n] = m
            t["up mm", n] = m

        def expert_tanh(n):
            act.wait(t["gate mm", n], t.get(("acted", n - 2)))
            t["th_f", n] = act.run(lambda e: e.activation(th_f[:, n % 2, :], GB[:, 0:IFP], ACT.Tanh, scale=0.5))

        def expert_act(n):
            dve.wait(t["th_f", n], t.get(("down mm", n - 2)), t["sorted clear"])
            m = dve.run(lambda e: e.scalar_tensor_tensor(th_f[:, n % 2, :], th_f[:, n % 2, :], 1.0, GB[:, 0:IFP],
                                                         ALU.add, ALU.mult))
            dve.wait(m, t["up mm", n])
            t["acted", n] = dve.run(lambda e: e.scalar_tensor_tensor(
                act_f[:, n % 2, :], th_f[:, n % 2, :], 0.5, UB[:, 0:IFP], ALU.mult, ALU.mult))

        def expert_down(n):
            w = n % NW
            pe.wait(t["acted", n], t["TB free"])
            for c in range(NCH):
                m = pe.run(lambda e, c=c: e.matmul(TB[:, 0:H], act_f[:, n % 2, c * P:(c + 1) * P], dn_w[:, w, c, :],
                                                   start=(c == 0), stop=(c == NCH - 1)), signal=c == NCH - 1)
            t["down mm", n] = m

        def expert_out(n):
            act.wait(t["down mm", n], t.get(("ys stored", n - 2)))
            t["TB free"] = act.run(lambda e: e.copy(ys[:, n % 2, :], TB[:, 0:H]))
            sp.wait(t["TB free"])
            t["ys stored", n] = dma(ffn_d[n * P:(n + 1) * P, :], ys[:, n % 2, :], "ysout", n % 2)

        def gather(b, k):
            k2 = b % 2
            pool.wait(t["ys stored", NTILE - 2], t["ys stored", NTILE - 1], t.get(("out stored", b - 2)),
                      t["xn stored"], t["xn2"], t["xn turned"])
            if ("gather", k2) not in fl:
                fl["gather", k2] = flow(f"dma_gather{k2}")
            t["gathered", b] = pool.run(lambda e: e.indirect_dma_start(
                out=fin[k2][:, k, :], out_offset=None, in_=ffn_d,
                in_offset=bass.IndirectOffsetOnAxis(ap=pos_u[:, b * KB + k:b * KB + k + 1], axis=0)),
                flow=fl["gather", k2], by=16)

        def final_load(b):
            k2 = b % 2
            sp.wait(t["attn stored", b], t.get(("out stored", b - 2)), t["scattered", NB - 2 + k2])
            t["attn in", b] = dma(attn_in[:, k2, :, :], by_batch(attn_d, b), "attnin", k2)

        def final(b):
            k2 = b % 2
            dve.wait(t["attn in", b], t["gathered", b])
            m = dve.run(lambda e: e.tensor_tensor(fin[k2][:, :, :], fin[k2][:, :, :], attn_in[:, k2, :, :], ALU.add))
            sp.wait(m)
            t["out stored", b] = dma(by_batch(out, b), fin[k2][:, :, :], "out", k2)

        def late_add(b):
            dve.wait(t["gathered", b], t["base in"])
            t["late in", b] = t["out stored", b] = dve.run(lambda e: e.tensor_tensor(
                base_in[:, :, :], base_in[:, :, :], fin[b % 2][:, :, :], ALU.add))

        later = {}

        def at(step, fn, *a):
            later.setdefault(step, []).append((fn, a))

        def front(v, s0=None):
            plan = [(-9, batch_turn, v // 2)] if v % 2 == 0 else []
            plan += [(-8, in_proj, v, 0, 0), (-6, in_proj, v, 0, 1), (-5, in_proj, v, 1, 0), (-3, in_proj, v, 1, 1),
                     (-5, xi_act, v, 0), (-3, xi_act, v, 1), (-2, xi_mul, v, 0), (1, xi_mul, v, 1),
                     (-5, z_proj, v, 0), (1, z_proj, v, 1), (0, z_act, v, 0), (2, z_act, v, 1),
                     (1, x_proj, v), (3, z_mul, v, 0), (4, z_mul, v, 1), (2, dbc_out, v),
                     (4, dt_proj, v), (3, BC_load, v), (5, softplus, v), (8, delta_out, v),
                     (10, pair_load, v, 0), (12, pair_load, v, 1)]
            for k, fn, *a in sorted(plan, key=lambda x: x[0]):
                if s0 is None and (fn, *a) == (pair_load, 0, 0):
                    first_pair()
                elif s0 is None:
                    fn(*a, *([dve] if fn is delta_out else []))
                else:
                    at(s0 + k if s0 or k > 8 else max(0, (k + 8) // 2), fn, *a)

        ln_first(0)
        ln_second(0)
        prepare_front()
        ln_third(0)
        prepare_A()
        prepare_rest()
        front(0)
        clear_sorted()
        for c, steps in [(1, LN_ONE)] + [(c, [LN_START + LN_GAP * (c - 2) + k for k in LN_MORE]) for c in range(2, NB)]:
            for k, fn in zip(steps, (ln_load, ln_first, ln_second, ln_third)):
                at(k, fn, c)
        for u in range(UNITS):
            s0 = NSTEP * u
            at(s0, pair_load, u, 2)
            at(s0 + 4, pair_load, u, 3)
            if u + 1 < UNITS:
                front(u + 1, s0)
                if u % 2 == 0 and u + 2 < UNITS:
                    at(s0 + 5, batch_load, (u + 2) // 2)
            at(s0 + 12, gate, u, 0)
            at(s0 + NSTEP + 4, gate, u, 1)
            if u % 2 == 1:
                b = u // 2
                at(s0 + NSTEP - 2, base_load, b)
                if b >= NB - LATE:
                    at(s0 + NSTEP + (7 if b < NB - 1 else 1), late_add, b)
                if b < NB - 1:
                    at(s0 + NSTEP + 5, bias_mm, b)
                    for i in range(4):
                        at(s0 + NSTEP + 5 + i, out_mm, b, i)
                    at(s0 + NSTEP + 12, out_add, b)
                else:
                    for k, fn, *a in ((13, bias_mm), (13, out_mm, 0), (13, out_mm, 1), (14, out_mm, 2),
                                      (NSTEP + 4, out_mm, 3), (NSTEP + 4, out_add)):
                        at(s0 + k, fn, b, *a)
        r0 = LN_START + LN_GAP * (NB - 3) + LN_MORE[-1] + 2
        at(r0, route)
        for c in range(NB):
            at(r0 + 2 + 2 * c, scatter_load, c)
            for k in range(KB):
                at(r0 + 3 + 2 * c + k // 2, scatter, c, k)
        f0, gap = r0 + 24, 3
        for n in range(NTILE):
            s0 = f0 + gap * n
            for k, fn in ((0, expert_load), (4, expert_turn), (4, expert_xT), (5, expert_up), (5, expert_tanh),
                          (8, expert_act), (8, expert_down), (9, expert_out)):
                at(s0 + k, fn, n)
        g0 = f0 + gap * NTILE + 11
        last = UNITS * NSTEP
        for b in range(NB):
            s0 = g0 + 4 * b if b >= NB - LATE else max(g0 + 4 * b, NSTEP * (2 * b + 2) + 10)
            for k in range(KB):
                at(s0 + k, gather, b, k)
            if b < NB - LATE:
                at(s0, final_load, b)
                at(s0 + 8, final, b)
        for m in range(LEAD):
            decay(0, m)
        du_B(0, 0)
        m = 0
        while m < last + SUM_LAG or any(k >= m for k in later):
            if m + LEAD < last:
                decay(*divmod(m + LEAD, NSTEP))
            for fn, a in later.get(m, ()):
                fn(*a)
            if m < last:
                u, s = divmod(m, NSTEP)
                if m + 1 < last and s % 2:
                    du_B(*divmod(m + 1, NSTEP))
                scan(u, s)
                times_C(u, s)
            if m >= SUM_LAG and (m - SUM_LAG) % 2 and m - SUM_LAG < last:
                u, s = divmod(m - SUM_LAG, NSTEP)
                if s % 8 == 1:
                    skip_mm(u, s // 8)
                sum_states(u, s)
            m += 1
        for name, f in list(fl.items()):
            sp.wait((f, f.value))

        block = ctx.enter_context(nc.Block())

        @block.sync
        def _(e):
            sp.play(e)

        @block.tensor
        def _(e):
            pe.play(e)

        @block.scalar
        def _(e):
            act.play(e)

        @block.vector
        def _(e):
            dve.play(e)

        @block.gpsimd
        def _(e):
            pool.play(e)


def shape_constants():
    import numpy as np
    c = np.zeros((P, C_END), np.float32)
    c[:, C_ID:C_ID + P] = np.eye(P)
    c[:, C_TRI:C_TRI + P] = np.triu(np.ones((P, P)), 1)
    c[:, C_SEL:C_SEL + DD] = np.tile(np.eye(DD), (G, 1))
    c[:, C_IOTA:C_IOTA + E] = np.arange(E)
    c[:, C_THR:C_THR + NBLK] = P * np.arange(NBLK)
    c[:, C_NOTFIRST:C_NOTFIRST + E * NBLK] = np.tile(np.arange(NBLK) > 0, E)
    c[:, C_TILE:C_TILE + NTILE] = np.arange(NTILE)
    return c


def kernel(**inputs):
    import numpy as np
    import concourse.bacc as bacc
    from concourse.bass_utils import run_bass_kernel_spmd

    a = {k: np.asarray(v) for k, v in inputs.items()}

    def both(name, lay):
        return np.ascontiguousarray(np.stack([lay(a[f"L0_attn_{d}_{name}"]) for d in "fb"]))

    def halves(v):
        return v.reshape(2, P).T

    gate_up = np.zeros((E, P, 2, IFP), np.float32)
    gate_up[:, :, 0, :IF] = a["L0_ffn_gate_w"].transpose(0, 2, 1)
    gate_up[:, :, 1, :IF] = a["L0_ffn_up_w"].transpose(0, 2, 1)
    down = np.zeros((E, IFP, H), np.float32)
    down[:, :IF] = a["L0_ffn_down_w"].transpose(0, 2, 1)
    arrays = {
        "x": a["L0_attn_x"].reshape(NBLK * P, H),
        "in_wT": both("in_w", lambda w: w.T).transpose(1, 0, 2),
        "conv_wT": both("conv_w", lambda w: w.T).reshape(2 * NTAP * DI),
        "x_wT": both("x_w", lambda w: w.T.reshape(2, P, NDBC).transpose(1, 0, 2)).transpose(1, 0, 2, 3),
        "dt_wT": both("dt_w", lambda w: w.T).transpose(1, 0, 2),
        "A_log": both("A_log", lambda w: w.reshape(J, DD, G, R).transpose(2, 1, 0, 3).reshape(P, J, R))
        .transpose(1, 0, 2, 3),
        "out_w": both("out_w", lambda w: w).transpose(1, 0, 2),
        "comb_wT": a["L0_attn_combine_w"].T.reshape(2, P, H).transpose(1, 0, 2),
        "comb_b": a["L0_attn_combine_b"].reshape(1, H),
        "col_vectors": np.concatenate(
            [both(n, halves).transpose(1, 0, 2).reshape(P, 4) for n in ("conv_b", "dt_b", "D")]
            + [a["L0_attn_ln_g"].reshape(P, 1), a["L0_attn_ln_b"].reshape(P, 1)], axis=1),
        "router_wT": a["L0_ffn_router_w"].T,
        "gate_up": gate_up.reshape(E, P, 2 * IFP),
        "down": down.reshape(E, NCH, P, H).transpose(0, 2, 1, 3).reshape(E, P, NCH * H),
        "consts": shape_constants(),
    }
    nc = bacc.Bacc("TRN2", target_bir_lowering=False, num_devices=1)
    fed, args = {}, []
    for name, v in arrays.items():
        v = np.ascontiguousarray(v)
        fed["in_" + name] = v
        args.append(nc.dram_tensor("in_" + name, v.shape, mybir.dt.from_np(v.dtype), kind="ExternalInput").ap())
    out = nc.dram_tensor("out_0", (NBLK * P, H), F32, kind="ExternalOutput").ap()
    mamba_moe_kernel(nc, *args, out)
    r = run_bass_kernel_spmd(nc, [fed], core_ids=[0])
    return r.results[0]["out_0"].reshape(NB, L, H)
```
